# Optimizing a Trainium2 kernel written in Bass

```python
import numpy as np
import jax
import jax.numpy as jnp

def _softmax(x, axis=-1):
    return jax.nn.softmax(x, axis=axis)

def _gelu(x):
    return jax.nn.gelu(x, approximate=True)

def _silu(x):
    return jax.nn.silu(x)

def _sigmoid(x):
    return jax.nn.sigmoid(x)

def _layernorm(x, axis=-1, eps=1e-05):
    m = jnp.mean(x, axis=axis, keepdims=True)
    v = jnp.var(x, axis=axis, keepdims=True)
    return (x - m) / jnp.sqrt(v + eps)

def _scatter_add(tgt, idx, src, axis=0):
    return tgt.at[idx].add(src)

def _segment_sum(src, seg, n):
    return jax.ops.segment_sum(src, seg, n)
kernel_name = 'mk_adaln_ffn_d1_seqx_r8_1b8680'

def setup_inputs(seed: int=0):
    np.random.seed(seed)
    _w = jnp.asarray

    def _rec_inputs():
        import jax
        import jax.numpy as jnp
        _rk = jax.random.key(seed)
        x = -0.000125 + 0.9999 * jax.random.normal(jax.random.fold_in(_rk, 1), (128, 32, 512), jnp.float32)
        _lenS = 32 - jax.random.randint(jax.random.fold_in(_rk, 7), (128,), 0, max(1, 32 // 4) + 1, jnp.int32)
        _lenS2 = 32 - jax.random.randint(jax.random.fold_in(_rk, 8), (128,), 0, max(1, 32 // 4) + 1, jnp.int32)
        itok_B_0_23 = jax.random.randint(jax.random.fold_in(_rk, 11), (128,), 0, 24, jnp.int32)
        return (x, itok_B_0_23)
    x, itok_B_0_23 = _rec_inputs()

    def _L0_cond_setup():
        import jax, jax.numpy as jnp
        import numpy as np
        R = 16
        ALPHA = 32
        SCALING = ALPHA / R
        SLOTS = 32
        IN_F = 512
        OUT_F = 512
        B, T = (8, 128)
        key = jax.random.key(seed)
        k1, k2, k3, k4, k5, k6 = jax.random.split(key, 6)
        x = jax.random.normal(k1, (B, T, IN_F), dtype=jnp.float32)
        adapter_mapping = jax.random.randint(k2, (B,), 0, SLOTS, dtype=jnp.int32)
        W = jax.random.normal(k3, (OUT_F, IN_F), dtype=jnp.float32) * 0.02
        b = jax.random.normal(k4, (OUT_F,), dtype=jnp.float32) * 0.02
        lora_As = jax.random.normal(k5, (SLOTS, IN_F, R), dtype=jnp.float32) * 0.02
        lora_Bs = jax.random.normal(k6, (SLOTS, R, OUT_F), dtype=jnp.float32) * 0.02
        return {'x': x, 'adapter_mapping': adapter_mapping, 'W': W, 'b': b, 'lora_As': lora_As, 'lora_Bs': lora_Bs}
    _L0_cond_all = _L0_cond_setup()
    _L0_cond_in = {k: v for k, v in _L0_cond_all.items() if k in ('W', 'b', 'lora_As', 'lora_Bs')}
    del _L0_cond_all

    def _L0_ffn_setup():
        import jax, jax.numpy as jnp
        import numpy as np
        HIDDEN = 512
        INTER = 1376
        GROUP = 128
        B, S = (4, 256)
        NIB = jnp.uint32(15)

        def _pack_rows(nib):
            r = nib.reshape(-1, 8, nib.shape[-1])
            shifts = (jnp.arange(8, dtype=jnp.uint32) * 4)[None, :, None]
            return jnp.sum(r << shifts, axis=1, dtype=jnp.uint32)

        def _pack_cols(nib):
            r = nib.reshape(nib.shape[0], -1, 8)
            shifts = (jnp.arange(8, dtype=jnp.uint32) * 4)[None, None, :]
            return jnp.sum(r << shifts, axis=2, dtype=jnp.uint32)

        def _dequant(qw, qz, sc, g_idx):
            shifts = jnp.arange(8, dtype=jnp.uint32) * 4
            wq = qw[:, None, :] >> shifts[None, :, None] & NIB
            wq = wq.reshape(-1, qw.shape[1]).astype(jnp.float32)
            zq = qz[:, :, None] >> shifts[None, None, :] & NIB
            zq = zq.reshape(qz.shape[0], -1).astype(jnp.float32) + 1.0
            return sc[g_idx] * (wq - zq[g_idx])
        key = jax.random.key(seed)
        ks = jax.random.split(key, 7)
        n_groups = HIDDEN // GROUP
        n_groups_d = INTER // GROUP
        x = jax.random.normal(ks[0], (B, S, HIDDEN), jnp.float32)
        nib_w_gu = jax.random.randint(ks[1], (HIDDEN, 2 * INTER), 0, 16).astype(jnp.uint32)
        nib_z_gu = jax.random.randint(ks[2], (n_groups, 2 * INTER), 0, 15).astype(jnp.uint32)
        qweight_gu = _pack_rows(nib_w_gu)
        qzeros_gu = _pack_cols(nib_z_gu)
        scales_gu = jax.random.uniform(ks[3], (n_groups, 2 * INTER), jnp.float32, 0.005, 0.02)
        g_idx_gu = jnp.arange(HIDDEN, dtype=jnp.int32) // GROUP
        nib_w_d = jax.random.randint(ks[4], (INTER, HIDDEN), 0, 16).astype(jnp.uint32)
        nib_z_d = jax.random.randint(ks[5], (n_groups_d, HIDDEN), 0, 15).astype(jnp.uint32)
        qweight_down = _pack_rows(nib_w_d)
        qzeros_down = _pack_cols(nib_z_d)
        scales_down = jax.random.uniform(ks[6], (n_groups_d, HIDDEN), jnp.float32, 0.005, 0.02)
        g_idx_down = jnp.arange(INTER, dtype=jnp.int32) // GROUP
        return {'x': x, 'qweight_gu': qweight_gu, 'qzeros_gu': qzeros_gu, 'scales_gu': scales_gu, 'g_idx_gu': g_idx_gu, 'qweight_down': qweight_down, 'qzeros_down': qzeros_down, 'scales_down': scales_down, 'g_idx_down': g_idx_down}
    _L0_ffn_all = _L0_ffn_setup()
    _L0_ffn_in = {k: v for k, v in _L0_ffn_all.items() if k in ('qweight_gu', 'qzeros_gu', 'scales_gu', 'g_idx_gu', 'qweight_down', 'qzeros_down', 'scales_down', 'g_idx_down')}
    del _L0_ffn_all
    return {'x': x, 'itok_B_0_23': itok_B_0_23, 'L0_cond_W': _L0_cond_in['W'], 'L0_cond_b': _L0_cond_in['b'], 'L0_cond_lora_As': _L0_cond_in['lora_As'], 'L0_cond_lora_Bs': _L0_cond_in['lora_Bs'], 'L0_ffn_qweight_gu': _L0_ffn_in['qweight_gu'], 'L0_ffn_qzeros_gu': _L0_ffn_in['qzeros_gu'], 'L0_ffn_scales_gu': _L0_ffn_in['scales_gu'], 'L0_ffn_g_idx_gu': _L0_ffn_in['g_idx_gu'], 'L0_ffn_qweight_down': _L0_ffn_in['qweight_down'], 'L0_ffn_qzeros_down': _L0_ffn_in['qzeros_down'], 'L0_ffn_scales_down': _L0_ffn_in['scales_down'], 'L0_ffn_g_idx_down': _L0_ffn_in['g_idx_down']}

def reference(x, itok_B_0_23, L0_cond_W, L0_cond_b, L0_cond_lora_As, L0_cond_lora_Bs, L0_ffn_qweight_gu, L0_ffn_qzeros_gu, L0_ffn_scales_gu, L0_ffn_g_idx_gu, L0_ffn_qweight_down, L0_ffn_qzeros_down, L0_ffn_scales_down, L0_ffn_g_idx_down):
    import jax
    import jax.numpy as jnp

    def _L0_cond_ref(x, adapter_mapping, W, b, lora_As, lora_Bs):
        import jax, jax.numpy as jnp
        import numpy as np
        R = 16
        ALPHA = 32
        SCALING = ALPHA / R
        SLOTS = 32
        IN_F = 512
        OUT_F = 512
        B, T = (8, 128)
        base_out = jnp.einsum('bti,oi->bto', x, W) + b
        A = lora_As[adapter_mapping]
        Bm = lora_Bs[adapter_mapping]
        lora_h = jnp.einsum('bti,bir->btr', x, A)
        lora_out = jnp.einsum('btr,bro->bto', lora_h, Bm)
        return base_out + lora_out * SCALING

    def _L0_ffn_ref(x, qweight_gu, qzeros_gu, scales_gu, g_idx_gu, qweight_down, qzeros_down, scales_down, g_idx_down):
        import jax, jax.numpy as jnp
        import numpy as np
        HIDDEN = 512
        INTER = 1376
        GROUP = 128
        B, S = (4, 256)
        NIB = jnp.uint32(15)

        def _pack_rows(nib):
            r = nib.reshape(-1, 8, nib.shape[-1])
            shifts = (jnp.arange(8, dtype=jnp.uint32) * 4)[None, :, None]
            return jnp.sum(r << shifts, axis=1, dtype=jnp.uint32)

        def _pack_cols(nib):
            r = nib.reshape(nib.shape[0], -1, 8)
            shifts = (jnp.arange(8, dtype=jnp.uint32) * 4)[None, None, :]
            return jnp.sum(r << shifts, axis=2, dtype=jnp.uint32)

        def _dequant(qw, qz, sc, g_idx):
            shifts = jnp.arange(8, dtype=jnp.uint32) * 4
            wq = qw[:, None, :] >> shifts[None, :, None] & NIB
            wq = wq.reshape(-1, qw.shape[1]).astype(jnp.float32)
            zq = qz[:, :, None] >> shifts[None, None, :] & NIB
            zq = zq.reshape(qz.shape[0], -1).astype(jnp.float32) + 1.0
            return sc[g_idx] * (wq - zq[g_idx])
        w_gu = _dequant(qweight_gu, qzeros_gu, scales_gu, g_idx_gu)
        inter = jnp.einsum('bsh,hf->bsf', x, w_gu)
        gate, up = (inter[..., :INTER], inter[..., INTER:])
        h = jax.nn.silu(gate) * up
        w_d = _dequant(qweight_down, qzeros_down, scales_down, g_idx_down)
        return jnp.einsum('bsf,fh->bsh', h, w_d)
    x = x + _L0_ffn_ref(_L0_cond_ref(x, itok_B_0_23, L0_cond_W, L0_cond_b, L0_cond_lora_As, L0_cond_lora_Bs), L0_ffn_qweight_gu, L0_ffn_qzeros_gu, L0_ffn_scales_gu, L0_ffn_g_idx_gu, L0_ffn_qweight_down, L0_ffn_qzeros_down, L0_ffn_scales_down, L0_ffn_g_idx_down)
    return x

_drawn_inputs = setup_inputs


def setup_inputs(seed=0):
    import zlib

    import numpy as np

    out = dict(_drawn_inputs(seed))
    spreads = {}
    factors = {}
    for name, (base, spread) in spreads.items():
        noise = np.random.default_rng([zlib.crc32(name.encode()), seed]).standard_normal(out[name].shape)
        drawn = base * np.exp(spread * noise) if base else spread * noise
        out[name] = jnp.asarray(drawn.astype(out[name].dtype))
    for name, factor in factors.items():
        out[name] = (out[name] * factor).astype(out[name].dtype)
    return out
```

```python
from contextlib import ExitStack

import concourse.bass as bass
from concourse import mybir

F32 = mybir.dt.float32
F32R = mybir.dt.float32r
BF16 = mybir.dt.bfloat16
I32 = mybir.dt.int32
U32 = mybir.dt.uint32
ALU = mybir.AluOpType
ACT = mybir.ActivationFunctionType
AX_X = mybir.AxisListType.X

P = 128
D = 512
KT = D // P
F = 1376
FT = -(-F // P)
BATCHES, T = 128, 32
SLOTS, R = 32, 16
TOKENS = BATCHES * T
TN = 512
NT = TOKENS // TN
TILE_BATCHES = TN // T
LB = P // R
LN = LB * T
LG = TN // LN
LORA_SCALE = 2.0
NIBBLES = 8
GU_GROUPS = D // P
D_GROUPS = F // P
BANKS = 4
HI, MID, LO = 0, 32, 64
PARTS = 96
ZERO_AHEAD = 4
Q_SLOTS = 2
RES_AT = 1
SPLIT_AT = 4
GATHER_SPLIT_AT = 6
LORA_AT = 8


def width(m):
    return min(P, F - m * P)


class BankOrder:

    def __init__(self):
        self.turn, self.fills, self.freed = 0, 0, [0] * BANKS
        self.parts = {}

    def add(self, part, names, repeats=1):
        if repeats > 1:
            names = names + [None] * (-len(names) % BANKS)
        places, uses, fills = {}, [0] * BANKS, 0
        for n, name in enumerate(names):
            bank = (self.turn + n) % BANKS
            if name is not None:
                fills += 1
                places[name] = (bank, self.fills + fills, self.freed[bank] + uses[bank])
                uses[bank] += 1
        self.parts[part] = (places, fills, uses)
        self.turn += len(names) * repeats
        self.fills += fills * repeats
        self.freed = [a + b * repeats for a, b in zip(self.freed, uses)]

    def bank(self, part, name):
        return self.parts[part][0][name][0]

    def filled(self, part, name, turn=0):
        places, fills, _ = self.parts[part]
        return turn * fills + places[name][1]

    def free(self, part, name, turn=0):
        places, _, uses = self.parts[part]
        bank, _, before = places[name]
        return turn * uses[bank] + before

    def taken(self, part, name, turn=0):
        return self.free(part, name, turn) + 1


def prologue_products(grouped):
    names = [("ranks",)]
    for j in range(KT):
        names.append(("cond", j))
        if grouped:
            names += [("zero", j, 0), ("zero", j, 1)]
    return names


def tile_products(grouped, part):
    names = []
    for m in range(FT):
        if part == "first":
            if grouped and m + ZERO_AHEAD < FT:
                names += [("zero", m + ZERO_AHEAD, 0), ("zero", m + ZERO_AHEAD, 1)]
            names += [("down zero", m), ("down scale", m)]
        for g in range(GU_GROUPS if grouped else 1):
            names += [("gate", m, g), ("up", m, g)]
        if m == LORA_AT and part != "last":
            names.append(("ranks",))
    if part != "last":
        names += [("cond", j) for j in range(KT)]
    return names


def bank_order(grouped):
    order = BankOrder()
    order.add("prologue", prologue_products(True))
    if not grouped:
        order.add("weights", [(what, m, half) for m in range(FT) for half in range(2)
                              for what in ("zero", "scale")])
    order.add("first", tile_products(grouped, "first"))
    order.add("loop", tile_products(grouped, "loop"), NT - 2)
    order.add("last", tile_products(grouped, "last"))
    return order


def adaln_ffn(nc, xT, slots, wcT, bias, lora_a, lora_b, q_gu, q_gu_tail, qz_gu, s_gu, s_gu_col,
              s_gu_col_tail, gidx_gu, q_d, qz_d, s_d, gidx_d, outT):
    with ExitStack() as ctx:
        def sb(name, shape, dt=F32):
            return ctx.enter_context(nc.sbuf_tensor(name, shape, dt))

        def sem(name):
            return ctx.enter_context(nc.semaphore(name))

        gu_w = sb("gu_w", [P, FT, 2, KT, P], F32R)
        d_hi = sb("d_hi", [P, FT, D], F32R)
        d_lo = sb("d_lo", [P, FT, D], F32R)
        wc_hi = sb("wc_hi", [P, KT, D], F32R)
        wc_lo = sb("wc_lo", [P, KT, D], F32R)
        x_in = sb("x_in", [P, KT, TN])
        x_hi = sb("x_hi", [P, KT, TN], F32R)
        x_lo = sb("x_lo", [P, KT, TN], F32R)
        res = sb("res", [P, KT, TN])
        y_hi = sb("y_hi", [P, KT, TN], F32R)
        y_lo = sb("y_lo", [P, KT, TN], F32R)
        a_in = sb("a_in", [P, TILE_BATCHES, KT * R])
        a_hi = sb("a_hi", [P, LG, KT, P], F32R)
        a_lo = sb("a_lo", [P, LG, KT, P], F32R)
        b_in = sb("b_in", [P, LG, D])
        b_hi = sb("b_hi", [P, LG, D], F32R)
        b_lo = sb("b_lo", [P, LG, D], F32R)
        mask = sb("mask", [P, LB, T], BF16)
        ranks = sb("ranks", [P, TN])
        ranks_hi = sb("ranks_hi", [P, TN], F32R)
        ranks_lo = sb("ranks_lo", [P, TN], F32R)
        acc = sb("acc", [P, 2, 2, TN])
        h_hi = sb("h_hi", [P, 2, TN], F32R)
        h_lo = sb("h_lo", [P, 2, TN], F32R)
        q_gu_sb = sb("q_gu_sb", [P, Q_SLOTS, 2 * KT * P], U32)
        q_d_sb = sb("q_d_sb", [P, D], U32)
        w_new = sb("w_new", [P, D])
        member = sb("member", [PARTS, D + F], BF16)
        z_gu = sb("z_gu", [GU_GROUPS, 2 * F], BF16)
        z_d = sb("z_d", [D_GROUPS, D], BF16)
        s_d_parts = sb("s_d_parts", [PARTS, D], BF16)
        s_col = sb("s_col", [P, FT, 2, GU_GROUPS])
        bias_sb = sb("bias_sb", [P, KT])
        shift = sb("shift", [P, 1], U32)
        group = sb("group", [P, 1])
        slots_sb = sb("slots_sb", [1, BATCHES], I32)
        odd_rows = sb("odd_rows", [1, 2])
        odd_rows_i = sb("odd_rows_i", [1, 1], I32)
        column = sb("column", [P, 2], I32)

        gidx_sb = res[:].rearrange("p k n -> p (k n)").bitcast(I32)[0:PARTS, 0:D + F]
        regular = w_new[0:1, :].bitcast(I32)
        qz_gu_sb = ranks[0:GU_GROUPS, 0:2 * F // NIBBLES].bitcast(U32)
        qz_d_sb = ranks[0:D_GROUPS, TN - D // NIBBLES:TN].bitcast(U32)
        spare = [acc[:, i // 2, i % 2, :] for i in range(4)]
        member_tmp = acc[:].rearrange("p a b n -> p (a b n)")[0:PARTS, 0:F]
        scale_in = spare[3][0:PARTS, :]
        scale_rest = spare[0].bitcast(BF16)[0:PARTS, 0:D]
        s_gu_parts = spare[1].bitcast(BF16)[0:PARTS, 0:P]

        ring = ctx.enter_context(nc.psum_tensor("ring", [P, BANKS, TN], F32))
        down_ps = ctx.enter_context(nc.psum_tensor("down_ps", [P, KT, TN], F32))

        wc_in = [q_gu_sb[:, k // 2, k % 2 * D:(k % 2 + 1) * D].bitcast(F32) for k in range(KT)]

        slots_loaded = sem("slots_loaded")
        gidx_gu_loaded = sem("gidx_gu_loaded")
        gidx_d_loaded = sem("gidx_d_loaded")
        qz_gu_loaded = sem("qz_gu_loaded")
        qz_d_loaded = sem("qz_d_loaded")
        s_d_loaded = sem("s_d_loaded")
        columns_loaded = sem("columns_loaded")
        wc_loaded = [sem(f"wc_loaded{k}") for k in range(KT)]
        x0_loaded = [sem(f"x0_loaded{k}") for k in range(KT)]
        x_loaded = sem("x_loaded")
        a_loaded = sem("a_loaded")
        b_loaded = sem("b_loaded")
        q_loaded = [sem(f"q_loaded{i}") for i in range(Q_SLOTS)]
        qd_loaded = sem("qd_loaded")
        s_gu_loaded = sem("s_gu_loaded")
        w_moved = sem("w_moved")
        out_stored = sem("out_stored")
        scale_in_cleared = sem("scale_in_cleared")
        indices_made = sem("indices_made")
        mask_made = sem("mask_made")
        dve_step = sem("dve_step")
        member_gu_made = sem("member_gu_made")
        member_d_made = sem("member_d_made")
        form_known = sem("form_known")
        zero_unpacked = sem("zero_unpacked")
        z_gu_made = sem("z_gu_made")
        z_d_made = sem("z_d_made")
        s_d_made = sem("s_d_made")
        s_gu_made = sem("s_gu_made")
        w_new_made = sem("w_new_made")
        wc_hi_made = sem("wc_hi_made")
        wc_lo_made = sem("wc_lo_made")
        d_hi_made = sem("d_hi_made")
        d_lo_made = sem("d_lo_made")
        x_hi_made = sem("x_hi_made")
        x_lo_made = sem("x_lo_made")
        res_made = sem("res_made")
        adapters_hi_made = sem("adapters_hi_made")
        adapters_lo_made = sem("adapters_lo_made")
        ranks_hi_made = sem("ranks_hi_made")
        ranks_lo_made = sem("ranks_lo_made")
        y_hi_made = sem("y_hi_made")
        silu_made = sem("silu_made")
        h_made = sem("h_made")
        h_hi_made = sem("h_hi_made")
        h_lo_made = sem("h_lo_made")
        h_used = sem("h_used")
        down_filled = sem("down_filled")
        out_made = sem("out_made")
        filled = sem("filled")
        taken = [sem(f"taken{b}") for b in range(BANKS)]

        orders = {form: bank_order(form) for form in (True, False)}

        def in_both_forms(engine, run):
            engine.wait_ge(form_known, 1)
            odd = engine.value_load(odd_rows_i[0:1, 0:1], min_val=0, max_val=D)
            with engine.If(odd < 1):
                run(True)
            with engine.Else():
                run(False)

        def all_tiles(engine, run):
            run(0, "first", 0)
            with engine.Fori(1, NT - 1) as t:
                run(t, "loop", t - 1)
            run(NT - 1, "last", 0)

        def columns_of(half, m):
            return slice(half * F + m * P, half * F + m * P + width(m))

        def packed(m):
            return q_gu_sb[:, :, 0:2 * KT * width(m)].rearrange("p s (h k n) -> p s h k n", h=2, k=KT)

        def side_by_side(ap, m):
            return ap.rearrange("p (k n) -> p k n", n=P)[:, :, 0:width(m)]

        def by_rank(ap):
            return ap.rearrange("p k (b r) -> p k b r", r=R)

        def by_slot(g):
            return a_in[:, g * LB:(g + 1) * LB, :].rearrange("p b (k r) -> p k b r", r=R)

        block = ctx.enter_context(nc.Block())

        @block.sync
        def _(sp):
            def load_x(t):
                sp.wait_ge(res_made, t)
                sp.dma_start(x_in[:], xT[:, bass.ds(t * TN, TN)].rearrange("(k p) n -> p k n", p=P)
                             ).then_inc(x_loaded, 16)

            def gather(t):
                for b in range(TILE_BATCHES):
                    slot = sp.value_load(slots_sb[0:1, bass.ds(t * TILE_BATCHES + b, 1)],
                                         min_val=0, max_val=SLOTS - 1)
                    sp.dma_start(a_in[:, b, :],
                                 lora_a[bass.ds(slot, 1)].rearrange("o p c -> (o p) c")
                                 ).then_inc(a_loaded, 16)
                    sp.dma_start(b_in[b % LB * R:(b % LB + 1) * R, b // LB, :],
                                 lora_b[bass.ds(slot, 1)].rearrange("o r n -> (o r) n")
                                 ).then_inc(b_loaded, 16)

            def load_q(n, m):
                src = q_gu[m] if m < FT - 1 else q_gu_tail
                words = src.shape[-1]
                sp.dma_start(q_gu_sb[:, n % Q_SLOTS, 0:words],
                             src.unsqueeze(1).to_broadcast([P // NIBBLES, NIBBLES, words])
                             ).then_inc(q_loaded[n % Q_SLOTS], 16)

            def wait_taken(order, part, name):
                sp.wait_ge(taken[order.bank(part, name)], order.taken(part, name))

            def load_q_down(order, m):
                if m >= 1:
                    wait_taken(order, "first", ("down zero", m - 1))
                rows = width(m) // NIBBLES
                src = q_d[m * P // NIBBLES:m * P // NIBBLES + rows, :]
                sp.dma_start(q_d_sb[0:width(m), :],
                             src.unsqueeze(1).to_broadcast([rows, NIBBLES, D])
                             ).then_inc(qd_loaded, 16)

            sp.dma_start(slots_sb[:], slots).then_inc(slots_loaded, 16)
            sp.dma_start(gidx_sb[:, 0:D], gidx_gu.to_broadcast([PARTS, D])).then_inc(gidx_gu_loaded, 16)
            for k in range(KT):
                sp.dma_start(x_in[:, k, :], xT[k * P:(k + 1) * P, 0:TN]).then_inc(x0_loaded[k], 16)
                sp.dma_start(wc_in[k], wcT[k * P:(k + 1) * P, :]).then_inc(wc_loaded[k], 16)
                if k == 0:
                    sp.dma_start(qz_gu_sb, qz_gu).then_inc(qz_gu_loaded, 16)
            sp.wait_ge(slots_loaded, 16)
            gather(0)
            sp.dma_start(gidx_sb[:, D:D + F], gidx_d.to_broadcast([PARTS, F])).then_inc(gidx_d_loaded, 16)
            sp.dma_start(qz_d_sb, qz_d).then_inc(qz_d_loaded, 16)
            sp.dma_start(bias_sb[:], bias).then_inc(columns_loaded, 16)
            sp.dma_start(s_col[:, 0:FT - 1, :, :], s_gu_col).then_inc(columns_loaded, 16)
            sp.dma_start(s_col[0:width(FT - 1), FT - 1, :, :], s_gu_col_tail).then_inc(columns_loaded, 16)
            sp.wait_ge(scale_in_cleared, 1)
            for part in (HI, MID, LO):
                sp.dma_start(scale_in[part:part + D_GROUPS, :], s_d).then_inc(s_d_loaded, 16)
            for m in range(ZERO_AHEAD):
                if m < Q_SLOTS:
                    sp.wait_ge(wc_lo_made, 2 * (m + 1))
                else:
                    wait_taken(orders[True], "prologue", ("zero", m - Q_SLOTS, 1))
                load_q(m, m)

            def tiles(grouped):
                order = orders[grouped]

                def q_part(m):
                    return "prologue" if m < ZERO_AHEAD else "first"

                if not grouped:
                    for m in range(FT):
                        if m < Q_SLOTS:
                            wait_taken(order, "prologue", ("zero", ZERO_AHEAD - Q_SLOTS + m, 1))
                        else:
                            wait_taken(order, "weights", ("zero", m - Q_SLOTS, 1))
                        load_q(ZERO_AHEAD + m, m)
                        for half in range(2):
                            i = 2 * m + half
                            if i == 0:
                                sp.wait_ge(s_d_made, 1)
                            else:
                                sp.wait_ge(s_gu_made, i)
                            for part in (HI, MID, LO):
                                sp.dma_start(scale_in[part:part + GU_GROUPS, 0:width(m)],
                                             s_gu[:, columns_of(half, m)]).then_inc(s_gu_loaded, 16)
                            sp.wait_ge(w_new_made, i + 1)
                            sp.dma_start(gu_w[:, m, half, :, 0:width(m)].bitcast(F32),
                                         w_new[:, 0:KT * width(m)].rearrange(
                                             "p (k n) -> p k n", k=KT)).then_inc(w_moved, 16)

                def tile(t, part, turn):
                    if part == "first":
                        for m in range(FT):
                            ahead = m + ZERO_AHEAD
                            if grouped and ahead < FT:
                                wait_taken(order, q_part(ahead - Q_SLOTS), ("zero", ahead - Q_SLOTS, 1))
                                load_q(ahead, ahead)
                            load_q_down(order, m)
                            if m == RES_AT:
                                load_x(1)
                            if m == GATHER_SPLIT_AT - 2:
                                sp.wait_ge(adapters_lo_made, LG + 1)
                                gather(1)
                    elif part == "loop":
                        load_x(t + 1)
                        sp.wait_ge(adapters_lo_made, (LG + 1) * (t + 1))
                        gather(t + 1)
                    for j in range(KT):
                        sp.wait_ge(out_made, KT * t + j + 1)
                        sp.dma_start(outT[j * P:(j + 1) * P, bass.ds(t * TN, TN)],
                                     res[:, j, :]).then_inc(out_stored, 16)

                all_tiles(sp, tile)
                sp.wait_ge(out_stored, 16 * KT * NT)

            in_both_forms(sp, tiles)

        @block.gpsimd
        def _(pool):
            pool.memset(scale_in, 0.0).then_inc(scale_in_cleared, 1)
            pool.iota(column[:, 0:1], [[0, 1]], base=0, channel_multiplier=1)
            pool.iota(column[:, 1:2], [[0, 1]], base=0, channel_multiplier=4)
            pool.iota(regular.rearrange("o (k p) -> o k p", p=P), [[1, KT], [0, P]], base=0,
                      channel_multiplier=0).then_inc(indices_made, 1)
            pool.memset(mask[:], LORA_SCALE).then_inc(mask_made, 1)
            pool.wait_ge(mask_made, 1)
            pool.affine_select(out=mask[:], in_=mask[:], compare_op=ALU.is_ge, fill=0.0, base=0,
                               pattern=[[-R, LB], [0, T]], channel_multiplier=1).then_inc(mask_made, 1)
            pool.wait_ge(mask_made, 2)
            pool.affine_select(out=mask[:], in_=mask[:], compare_op=ALU.is_ge, fill=0.0, base=R - 1,
                               pattern=[[R, LB], [0, T]], channel_multiplier=-1).then_inc(mask_made, 1)

            def adapters_low(t):
                for g in range(LG):
                    pool.wait_ge(adapters_hi_made, (LG + 1) * t + g + 1)
                    pool.tensor_tensor(by_rank(a_lo[:, g]), by_slot(g), by_rank(a_hi[:, g].bitcast(F32)),
                                       ALU.subtract).then_inc(adapters_lo_made, 1)
                pool.wait_ge(adapters_hi_made, (LG + 1) * (t + 1))
                pool.tensor_tensor(b_lo[:], b_in[:], b_hi[:].bitcast(F32),
                                   ALU.subtract).then_inc(adapters_lo_made, 1)

            def ranks_low(t):
                pool.wait_ge(ranks_hi_made, t + 1)
                pool.tensor_tensor(ranks_lo[:], ranks[:], ranks_hi[:].bitcast(F32),
                                   ALU.subtract).then_inc(ranks_lo_made, 1)

            adapters_low(0)
            ranks_low(0)

            def tiles(grouped):
                order = orders[grouped]

                def product(t, part, turn, m):
                    a = acc[0:width(m), m % 2]
                    name = ("up", m, GU_GROUPS - 1)
                    pool.wait_ge(silu_made, FT * t + m + 1)
                    pool.wait_ge(taken[order.bank(part, name)], order.taken(part, name, turn))
                    pool.tensor_tensor(a[:, 1], a[:, 0], a[:, 1], ALU.mult).then_inc(h_made, 1)

                def h_low(t, m):
                    n = width(m)
                    pool.wait_ge(h_hi_made, FT * t + m + 1)
                    pool.tensor_tensor(h_lo[0:n, m % 2], acc[0:n, m % 2, 1], h_hi[0:n, m % 2].bitcast(F32),
                                       ALU.subtract).then_inc(h_lo_made, 1)

                def tile(t, part, turn):
                    for m in range(FT):
                        if m >= 1:
                            h_low(t, m - 1)
                        if part == "first":
                            n = width(m)
                            pool.wait_ge(d_hi_made, m + 1)
                            pool.tensor_tensor(d_lo[0:n, m], w_new[0:n], d_hi[0:n, m].bitcast(F32),
                                               ALU.subtract).then_inc(d_lo_made, 1)
                        if part != "last" and m == GATHER_SPLIT_AT:
                            adapters_low(t + 1)
                        if grouped:
                            product(t, part, turn, m)
                        if part != "last" and m == LORA_AT:
                            ranks_low(t + 1)
                    h_low(t, FT - 1)

                all_tiles(pool, tile)

            in_both_forms(pool, tiles)

        @block.scalar
        def _(act):
            def adapters_high(t):
                act.wait_ge(a_loaded, 16 * TILE_BATCHES * (t + 1))
                for g in range(LG):
                    act.activation(by_rank(a_hi[:, g]), by_slot(g), ACT.Copy).then_inc(adapters_hi_made, 1)
                act.wait_ge(b_loaded, 16 * TILE_BATCHES * (t + 1))
                act.activation(b_hi[:], b_in[:], ACT.Copy).then_inc(adapters_hi_made, 1)

            def ranks_high(order, part, turn, t):
                bank = order.bank(part, ("ranks",))
                act.wait_ge(taken[bank], order.taken(part, ("ranks",), turn))
                act.activation(ranks_hi[:], ranks[:], ACT.Copy).then_inc(ranks_hi_made, 1)

            def cond_high(order, part, turn, j):
                act.wait_ge(filled, order.filled(part, ("cond", j), turn))
                act.activation(y_hi[:, j, :], ring[:, order.bank(part, ("cond", j)), :], ACT.Identity,
                               bias=bias_sb[:, j:j + 1]).then_inc(y_hi_made, 1)

            for k in range(KT):
                act.wait_ge(x0_loaded[k], 16)
                act.activation(x_hi[:, k, :], x_in[:, k, :], ACT.Copy).then_inc(x_hi_made, 1)
                act.wait_ge(wc_loaded[k], 16)
                act.activation(wc_hi[:, k, :], wc_in[k], ACT.Copy).then_inc(wc_hi_made, 1)
            for n in range(NIBBLES):
                act.wait_ge(zero_unpacked, n + 1)
                act.activation(z_gu[:, n:2 * F:NIBBLES],
                               spare[n % 3].bitcast(U32)[0:GU_GROUPS, 0:2 * F // NIBBLES],
                               ACT.Copy, bias=1.0).then_inc(z_gu_made, 1)
            adapters_high(0)
            ranks_high(orders[True], "prologue", 0, 0)
            act.wait_ge(columns_loaded, 48)
            for j in range(KT):
                cond_high(orders[True], "prologue", 0, j)

            def tiles(grouped):
                order = orders[grouped]

                def start_group(t, part, turn, m, half):
                    name = (("gate", "up")[half], m, 0)
                    bank, n = order.bank(part, name), width(m)
                    act.wait_ge(filled, order.filled(part, name, turn))
                    act.activation(acc[0:n, m % 2, half], ring[0:n, bank, :], ACT.Copy,
                                   scale=s_col[0:n, m, half, 0:1]).then_inc(taken[bank], 1)

                def acc_free(t, part, m):
                    if m >= 2:
                        act.wait_ge(h_lo_made, FT * t + m - 1)
                    elif part != "first":
                        act.wait_ge(h_lo_made, FT * t)

                def silu(t, part, turn, m):
                    a = acc[0:width(m), m % 2, 0]
                    if grouped:
                        name = ("gate", m, GU_GROUPS - 1)
                        act.wait_ge(taken[order.bank(part, name)], order.taken(part, name, turn))
                        act.activation(a, a, ACT.Silu).then_inc(silu_made, 1)
                    else:
                        name = ("gate", m, 0)
                        bank = order.bank(part, name)
                        act.wait_ge(filled, order.filled(part, name, turn))
                        act.activation(a, ring[0:width(m), bank, :], ACT.Silu).then_inc(taken[bank], 1)

                def h_high(t, part, turn, m):
                    n = width(m)
                    if grouped:
                        act.wait_ge(h_made, FT * t + m + 1)
                    else:
                        name = ("up", m, 0)
                        act.wait_ge(taken[order.bank(part, name)], order.taken(part, name, turn))
                    if m >= 2:
                        act.wait_ge(h_used, (FT - 1) * t + m - 1)
                    elif part != "first":
                        act.wait_ge(down_filled, KT * t)
                    act.activation(h_hi[0:n, m % 2], acc[0:n, m % 2, 1], ACT.Copy).then_inc(h_hi_made, 1)

                def copy_residual(t, part):
                    act.wait_ge(x_lo_made, KT * (t + 1))
                    if part == "first":
                        act.wait_ge(member_d_made, 1)
                    else:
                        act.wait_ge(out_stored, 16 * KT * t)
                    for k in range(KT):
                        c = act.activation(res[:, k, :], x_in[:, k, :], ACT.Copy)
                    c.then_inc(res_made, 1)

                def tile(t, part, turn):
                    for m in range(FT):
                        acc_free(t, part, m)
                        if grouped:
                            for half in range(2):
                                start_group(t, part, turn, m, half)
                        if m >= 1:
                            h_high(t, part, turn, m - 1)
                        if part == "first":
                            n, name = width(m), ("down scale", m)
                            act.wait_ge(taken[order.bank(part, name)], order.taken(part, name))
                            act.activation(d_hi[0:n, m], w_new[0:n], ACT.Copy).then_inc(d_hi_made, 1)
                        if m == RES_AT:
                            copy_residual(t, part)
                        if part != "last" and SPLIT_AT <= m < SPLIT_AT + KT:
                            k = m - SPLIT_AT
                            act.wait_ge(x_loaded, 16 * (t + 1))
                            act.activation(x_hi[:, k, :], x_in[:, k, :], ACT.Copy).then_inc(x_hi_made, 1)
                        if part != "last" and m == GATHER_SPLIT_AT:
                            adapters_high(t + 1)
                        silu(t, part, turn, m)
                        if part != "last" and m == LORA_AT:
                            ranks_high(order, part, turn, t + 1)
                    h_high(t, part, turn, FT - 1)
                    if part != "last":
                        for j in range(KT):
                            cond_high(order, part, turn, j)

                all_tiles(act, tile)

            in_both_forms(act, tiles)

        @block.vector
        def _(dve):
            steps = [0]

            def settle(instruction):
                steps[0] += 1
                instruction.then_inc(dve_step, 1)
                dve.wait_ge(dve_step, steps[0])

            def make_member(columns, groups, made):
                idx, tmp = gidx_sb[:, columns], member_tmp[:, 0:columns.stop - columns.start]
                settle(dve.tensor_scalar(tmp, idx, 0.0, float(groups), ALU.is_lt, ALU.mult))
                settle(dve.tensor_tensor(tmp, idx, tmp, ALU.add))
                settle(dve.tensor_scalar(tmp, tmp, 0.0, float(groups - 1), ALU.max, ALU.min))
                dve.tensor_scalar(member[:, columns], tmp, group[0:PARTS, 0:1], None,
                                  ALU.is_equal).then_inc(made, 1)
                dve.wait_ge(made, 1)

            def split_scale(parts, made):
                n = parts.shape[-1]
                rest, s = scale_rest[:, 0:n], scale_in[:, 0:n]
                settle(dve.tensor_copy(parts, s))
                settle(dve.tensor_tensor(s, s, parts, ALU.subtract))
                settle(dve.tensor_copy(rest, s))
                settle(dve.tensor_copy(parts[MID:LO], rest[MID:LO]))
                settle(dve.tensor_tensor(s, s, rest, ALU.subtract))
                dve.tensor_copy(parts[LO:PARTS], s[LO:PARTS]).then_inc(made, 1)

            def unpack(q):
                settle(dve.tensor_scalar(q, q, shift[0:q.shape[0], 0:1], 15,
                                         ALU.logical_shift_right, ALU.bitwise_and))

            def x_low(k):
                dve.tensor_tensor(x_lo[:, k, :], x_in[:, k, :], x_hi[:, k, :].bitcast(F32),
                                  ALU.subtract).then_inc(x_lo_made, 1)

            def zero_weights(order, part, m):
                slot = m % Q_SLOTS
                dve.wait_ge(q_loaded[slot], 16 * (m // Q_SLOTS + 1))
                unpack(q_gu_sb[:, slot, 0:2 * KT * width(m)])
                for half in range(2):
                    bank = order.bank(part, ("zero", m, half))
                    dve.wait_ge(filled, order.filled(part, ("zero", m, half)))
                    dve.tensor_tensor(gu_w[:, m, half, :, 0:width(m)], packed(m)[:, slot, half],
                                      side_by_side(ring[:, bank, :], m),
                                      ALU.subtract).then_inc(taken[bank], 1)

            def take_ranks(order, part, turn, t):
                bank = order.bank(part, ("ranks",))
                if part != "prologue":
                    dve.wait_ge(ranks_lo_made, t)
                dve.wait_ge(filled, order.filled(part, ("ranks",), turn))
                for g in range(LG):
                    r = dve.tensor_tensor(ranks[:, g * LN:(g + 1) * LN], ring[:, bank, g * LN:(g + 1) * LN],
                                          mask[:].rearrange("p b t -> p (b t)"), ALU.mult)
                r.then_inc(taken[bank], 1)

            def cond_low(order, part, turn, t, j):
                bank = order.bank(part, ("cond", j))
                dve.wait_ge(y_hi_made, KT * t + j + 1)
                dve.scalar_tensor_tensor(y_lo[:, j, :], ring[:, bank, :], bias_sb[:, j:j + 1],
                                         y_hi[:, j, :].bitcast(F32), ALU.add,
                                         ALU.subtract).then_inc(taken[bank], 1)

            dve.wait_ge(indices_made, 1)
            settle(dve.tensor_scalar(column[:, 0:1], column[:, 0:1], 31, None, ALU.bitwise_and))
            dve.tensor_copy(group[:], column[:, 0:1])
            settle(dve.tensor_scalar(shift[:], column[:, 1:2].bitcast(U32), 4 * (NIBBLES - 1), None,
                                     ALU.bitwise_and))
            dve.wait_ge(gidx_gu_loaded, 16)
            make_member(slice(0, D), GU_GROUPS, member_gu_made)
            settle(dve.tensor_tensor(member_tmp[0:1, 0:D], member_tmp[0:1, 0:D], regular, ALU.not_equal))
            settle(dve.reduce_sum(odd_rows[:, 0:1], member_tmp[0:1, 0:D], axis=AX_X))
            dve.tensor_copy(odd_rows_i[:], odd_rows[:, 0:1]).then_inc(form_known, 1)

            for k in range(KT):
                dve.wait_ge(x_hi_made, k + 1)
                x_low(k)
                dve.wait_ge(wc_hi_made, k + 1)
                dve.tensor_tensor(wc_lo[:, k, :], wc_in[k], wc_hi[:, k, :].bitcast(F32),
                                  ALU.subtract).then_inc(wc_lo_made, 1)

            dve.wait_ge(qz_gu_loaded, 16)
            for n in range(NIBBLES):
                if n >= 3:
                    dve.wait_ge(z_gu_made, n - 2)
                dve.tensor_scalar(spare[n % 3].bitcast(U32)[0:GU_GROUPS, 0:2 * F // NIBBLES],
                                  qz_gu_sb, 4 * n, 15, ALU.logical_shift_right,
                                  ALU.bitwise_and).then_inc(zero_unpacked, 1)
            dve.wait_ge(z_gu_made, NIBBLES)

            dve.wait_ge(gidx_d_loaded, 16)
            make_member(slice(D, D + F), D_GROUPS, member_d_made)
            dve.wait_ge(qz_d_loaded, 16)
            z_tmp = spare[0].bitcast(U32)[0:D_GROUPS, :].rearrange("g (c n) -> g c n", n=NIBBLES)
            for n in range(NIBBLES):
                z = dve.tensor_scalar(z_tmp[:, :, n], qz_d_sb, 4 * n, 15, ALU.logical_shift_right,
                                      ALU.bitwise_and)
            settle(z)
            settle(dve.tensor_scalar(z_d[:], spare[0].bitcast(U32)[0:D_GROUPS, :], 1.0, None, ALU.add))
            dve.wait_ge(s_d_loaded, 48)
            split_scale(s_d_parts[:], s_d_made)

            dve.wait_ge(mask_made, 3)
            take_ranks(orders[True], "prologue", 0, 0)
            dve.wait_ge(columns_loaded, 48)
            for j in range(KT):
                cond_low(orders[True], "prologue", 0, 0, j)
                zero_weights(orders[True], "prologue", j)

            def tiles(grouped):
                order = orders[grouped]

                if not grouped:
                    for m in range(FT):
                        n, load = width(m), ZERO_AHEAD + m
                        slot = load % Q_SLOTS
                        dve.wait_ge(q_loaded[slot], 16 * (load // Q_SLOTS + 1))
                        unpack(q_gu_sb[:, slot, 0:2 * KT * n])
                        for half in range(2):
                            i = 2 * m + half
                            dve.wait_ge(s_gu_loaded, 48 * (i + 1))
                            split_scale(s_gu_parts[:, 0:n], s_gu_made)
                            if i >= 1:
                                dve.wait_ge(w_moved, 16 * i)
                            w = w_new[:, 0:KT * n].rearrange("p (k n) -> p k n", k=KT)
                            zero = order.bank("weights", ("zero", m, half))
                            dve.wait_ge(filled, order.filled("weights", ("zero", m, half)))
                            dve.tensor_tensor(w, packed(m)[:, slot, half], side_by_side(ring[:, zero, :], m),
                                              ALU.subtract).then_inc(taken[zero], 1)
                            scale = order.bank("weights", ("scale", m, half))
                            dve.wait_ge(taken[zero], order.taken("weights", ("zero", m, half)))
                            dve.wait_ge(filled, order.filled("weights", ("scale", m, half)))
                            settle(dve.tensor_tensor(w, w, side_by_side(ring[:, scale, :], m), ALU.mult))
                            dve.tensor_copy(odd_rows[:, 1:2], odd_rows[:, 0:1]).then_inc(taken[scale], 1)
                            dve.tensor_copy(odd_rows[:, 1:2], odd_rows[:, 0:1]).then_inc(w_new_made, 1)

                def down_weights(m):
                    n = width(m)
                    zero, scale = [order.bank("first", (what, m)) for what in ("down zero", "down scale")]
                    dve.wait_ge(qd_loaded, 16 * (m + 1))
                    unpack(q_d_sb[0:n, :])
                    if m >= 1:
                        dve.wait_ge(d_lo_made, m)
                    elif not grouped:
                        dve.wait_ge(w_moved, 16 * 2 * FT)
                    dve.wait_ge(filled, order.filled("first", ("down zero", m)))
                    dve.tensor_tensor(w_new[0:n], q_d_sb[0:n], ring[0:n, zero, :],
                                      ALU.subtract).then_inc(taken[zero], 1)
                    dve.wait_ge(taken[zero], order.taken("first", ("down zero", m)))
                    dve.wait_ge(filled, order.filled("first", ("down scale", m)))
                    dve.tensor_tensor(w_new[0:n], w_new[0:n], ring[0:n, scale, :],
                                      ALU.mult).then_inc(taken[scale], 1)

                def add_group(part, turn, m, half, g):
                    what, n = ("gate", "up")[half], width(m)
                    bank, last = order.bank(part, (what, m, g)), order.bank(part, (what, m, g - 1))
                    a = acc[0:n, m % 2, half]
                    dve.wait_ge(taken[last], order.taken(part, (what, m, g - 1), turn))
                    dve.wait_ge(filled, order.filled(part, (what, m, g), turn))
                    dve.scalar_tensor_tensor(a, ring[0:n, bank, :], s_col[0:n, m, half, g:g + 1], a,
                                             ALU.mult, ALU.add).then_inc(taken[bank], 1)

                def product(part, turn, m):
                    n = width(m)
                    gate, up = [order.bank(part, (what, m, 0)) for what in ("gate", "up")]
                    dve.wait_ge(taken[gate], order.taken(part, ("gate", m, 0), turn))
                    dve.wait_ge(filled, order.filled(part, ("up", m, 0), turn))
                    dve.tensor_tensor(acc[0:n, m % 2, 1], acc[0:n, m % 2, 0], ring[0:n, up, :],
                                      ALU.mult).then_inc(taken[up], 1)

                def tile(t, part, turn):
                    for m in range(FT):
                        if part == "first":
                            if grouped and m + ZERO_AHEAD < FT:
                                zero_weights(order, "first", m + ZERO_AHEAD)
                            down_weights(m)
                        if grouped:
                            for g in range(1, GU_GROUPS):
                                for half in range(2):
                                    add_group(part, turn, m, half, g)
                        else:
                            product(part, turn, m)
                        if part != "last" and SPLIT_AT <= m < SPLIT_AT + KT:
                            k = m - SPLIT_AT
                            dve.wait_ge(x_hi_made, KT * (t + 1) + k + 1)
                            x_low(k)
                        if part != "last" and m == LORA_AT:
                            take_ranks(order, part, turn, t + 1)
                    if part != "last":
                        for j in range(KT):
                            cond_low(order, part, turn, t + 1, j)
                    dve.wait_ge(res_made, t + 1)
                    for j in range(KT):
                        dve.wait_ge(down_filled, KT * t + j + 1)
                        dve.tensor_tensor(res[:, j, :], res[:, j, :], down_ps[:, j, :],
                                          ALU.add).then_inc(out_made, 1)

                all_tiles(dve, tile)

            in_both_forms(dve, tiles)

        @block.tensor
        def _(pe):
            def wait_free(order, part, name, turn=0):
                bank, before = order.bank(part, name), order.free(part, name, turn)
                if not (isinstance(before, int) and before == 0):
                    pe.wait_ge(taken[bank], before)
                return bank

            def split_product(out, w_hi, w_lo, v_hi, v_lo, start, stop):
                pe.matmul(out, w_hi, v_hi, start=start, stop=False)
                pe.matmul(out, w_hi, v_lo, start=False, stop=False)
                return pe.matmul(out, w_lo, v_hi, start=False, stop=stop)

            def ranks_product(order, part, turn, t):
                bank = wait_free(order, part, ("ranks",), turn)
                pe.wait_ge(x_lo_made, KT * (t + 1))
                for g in range(LG):
                    pe.wait_ge(adapters_lo_made, (LG + 1) * t + g + 1)
                    tokens = slice(g * LN, (g + 1) * LN)
                    for k in range(KT):
                        mm = split_product(ring[:, bank, tokens], a_hi[:, g, k], a_lo[:, g, k],
                                           x_hi[:, k, tokens], x_lo[:, k, tokens], k == 0, k == KT - 1)
                mm.then_inc(filled, 1)

            def cond_product(order, part, turn, t, j):
                bank = wait_free(order, part, ("cond", j), turn)
                columns = slice(j * P, (j + 1) * P)
                if j == 0:
                    pe.wait_ge(ranks_lo_made, t + 1)
                    pe.wait_ge(adapters_lo_made, (LG + 1) * (t + 1))
                for k in range(KT):
                    mm = split_product(ring[:, bank, :], wc_hi[:, k, columns], wc_lo[:, k, columns],
                                       x_hi[:, k, :], x_lo[:, k, :], k == 0, k == KT - 1)
                    if k == 0:
                        for g in range(LG):
                            tokens = slice(g * LN, (g + 1) * LN)
                            split_product(ring[:, bank, tokens], b_hi[:, g, columns], b_lo[:, g, columns],
                                          ranks_hi[:, tokens], ranks_lo[:, tokens], False, False)
                mm.then_inc(filled, 1)

            def zero_product(order, part, m, half):
                bank = wait_free(order, part, ("zero", m, half))
                for k in range(KT):
                    mm = pe.matmul(ring[:, bank, k * P:k * P + width(m)],
                                   member[0:GU_GROUPS, k * P:(k + 1) * P], z_gu[:, columns_of(half, m)],
                                   start=True, stop=True)
                mm.then_inc(filled, 1)

            pe.wait_ge(wc_lo_made, KT)
            ranks_product(orders[True], "prologue", 0, 0)
            for j in range(KT):
                cond_product(orders[True], "prologue", 0, 0, j)
                if j == 0:
                    pe.wait_ge(member_gu_made, 1)
                    pe.wait_ge(z_gu_made, NIBBLES)
                for half in range(2):
                    zero_product(orders[True], "prologue", j, half)

            def wait_y(order, part, turn):
                for j in range(KT):
                    pe.wait_ge(taken[order.bank(part, ("cond", j))], order.taken(part, ("cond", j), turn))

            def tiles(grouped):
                order = orders[grouped]
                wait_y(orders[True], "prologue", 0)

                if not grouped:
                    for m in range(FT):
                        for half in range(2):
                            zero_product(order, "weights", m, half)
                            bank = wait_free(order, "weights", ("scale", m, half))
                            pe.wait_ge(s_gu_made, 2 * m + half + 1)
                            for k in range(KT):
                                mm = pe.matmul(ring[:, bank, k * P:k * P + width(m)],
                                               member[:, k * P:(k + 1) * P], s_gu_parts[:, 0:width(m)],
                                               start=True, stop=True)
                            mm.then_inc(filled, 1)
                    pe.wait_ge(w_moved, 16 * 2 * FT)

                def down_weight_products(m):
                    rows = slice(D + m * P, D + m * P + width(m))
                    bank = wait_free(order, "first", ("down zero", m))
                    if m == 0:
                        pe.wait_ge(member_d_made, 1)
                        pe.wait_ge(s_d_made, 1)
                    pe.matmul(ring[0:width(m), bank, :], member[0:D_GROUPS, rows], z_d[:],
                              start=True, stop=True).then_inc(filled, 1)
                    bank = wait_free(order, "first", ("down scale", m))
                    pe.matmul(ring[0:width(m), bank, :], member[:, rows], s_d_parts[:],
                              start=True, stop=True).then_inc(filled, 1)

                def group_product(part, turn, m, half, g):
                    name, n = (("gate", "up")[half], m, g), width(m)
                    bank = wait_free(order, part, name, turn)
                    w = gu_w[:, m, half, g, 0:n]
                    pe.matmul(ring[0:n, bank, :], w, y_hi[:, g, :], start=True, stop=False)
                    pe.matmul(ring[0:n, bank, :], w, y_lo[:, g, :], start=False,
                              stop=True).then_inc(filled, 1)

                def general_product(part, turn, m, half):
                    name, n = (("gate", "up")[half], m, 0), width(m)
                    bank = wait_free(order, part, name, turn)
                    for k in range(KT):
                        w = gu_w[:, m, half, k, 0:n].bitcast(F32)
                        pe.matmul(ring[0:n, bank, :], w, y_hi[:, k, :].bitcast(F32),
                                  start=(k == 0), stop=False)
                        mm = pe.matmul(ring[0:n, bank, :], w, y_lo[:, k, :].bitcast(F32),
                                       start=False, stop=(k == KT - 1))
                    mm.then_inc(filled, 1)

                def down_product(t, part, m, js):
                    n = width(m)
                    if js[0] == 0:
                        pe.wait_ge(h_lo_made, FT * t + m + 1)
                        if part == "first":
                            pe.wait_ge(d_lo_made, m + 1)
                    for j in js:
                        columns = slice(j * P, (j + 1) * P)
                        if m == 0 and part != "first":
                            pe.wait_ge(out_made, KT * (t - 1) + j + 1)
                        mm = split_product(down_ps[:, j, :], d_hi[0:n, m, columns], d_lo[0:n, m, columns],
                                           h_hi[0:n, m % 2], h_lo[0:n, m % 2], m == 0, m == FT - 1)
                        if m == FT - 1:
                            mm.then_inc(down_filled, 1)
                    if m < FT - 1 and js[-1] == KT - 1:
                        mm.then_inc(h_used, 1)

                def tile(t, part, turn):
                    for m in range(FT):
                        if part == "first":
                            if grouped and m + ZERO_AHEAD < FT:
                                for half in range(2):
                                    if grouped:
                                        zero_product(order, "first", m + ZERO_AHEAD, half)
                            down_weight_products(m)
                            if grouped:
                                gu_part = "prologue" if m < ZERO_AHEAD else "first"
                                for half in range(2):
                                    name = ("zero", m, half)
                                    pe.wait_ge(taken[order.bank(gu_part, name)],
                                               order.taken(gu_part, name))
                        if grouped:
                            for g in range(GU_GROUPS):
                                for half in range(2):
                                    group_product(part, turn, m, half, g)
                                if g % 2 and m >= 2:
                                    down_product(t, part, m - 2, [g - 1, g])
                        else:
                            for half in range(2):
                                general_product(part, turn, m, half)
                            if m >= 2:
                                down_product(t, part, m - 2, [0, 1, 2, 3])
                        if part != "last" and m == LORA_AT:
                            ranks_product(order, part, turn, t + 1)
                    down_product(t, part, FT - 2, [0, 1, 2, 3])
                    if part != "last":
                        for j in range(KT):
                            cond_product(order, part, turn, t + 1, j)
                    down_product(t, part, FT - 1, [0, 1, 2, 3])
                    if part != "last":
                        wait_y(order, part, turn)

                all_tiles(pe, tile)

            in_both_forms(pe, tiles)


def kernel(**inputs):
    import numpy as np
    import concourse.bacc as bacc
    from concourse.bass_utils import run_bass_kernel_spmd

    a = {name: np.asarray(v) for name, v in inputs.items()}
    full = (FT - 1) * P
    q_gu = a["L0_ffn_qweight_gu"].reshape(KT, P // NIBBLES, 2, F).transpose(1, 2, 0, 3)
    s_gu = a["L0_ffn_scales_gu"].reshape(GU_GROUPS, 2, F)
    arrays = {
        "xT": a["x"].reshape(TOKENS, D).T,
        "slots": a["itok_B_0_23"].reshape(1, BATCHES),
        "wcT": a["L0_cond_W"].T,
        "bias": a["L0_cond_b"].reshape(KT, P).T,
        "lora_a": a["L0_cond_lora_As"].reshape(SLOTS, KT, P, R).transpose(0, 2, 1, 3).reshape(
            SLOTS, P, KT * R),
        "lora_b": a["L0_cond_lora_Bs"],
        "q_gu": q_gu[..., :full].reshape(P // NIBBLES, 2, KT, FT - 1, P).transpose(3, 0, 1, 2, 4).reshape(
            FT - 1, P // NIBBLES, 2 * KT * P),
        "q_gu_tail": q_gu[..., full:].reshape(P // NIBBLES, -1),
        "qz_gu": a["L0_ffn_qzeros_gu"],
        "s_gu": a["L0_ffn_scales_gu"],
        "s_gu_col": s_gu[..., :full].reshape(GU_GROUPS, 2, FT - 1, P).transpose(3, 2, 1, 0),
        "s_gu_col_tail": s_gu[..., full:].transpose(2, 1, 0),
        "gidx_gu": a["L0_ffn_g_idx_gu"].reshape(1, D),
        "q_d": a["L0_ffn_qweight_down"],
        "qz_d": a["L0_ffn_qzeros_down"],
        "s_d": a["L0_ffn_scales_down"],
        "gidx_d": a["L0_ffn_g_idx_down"].reshape(1, F),
    }
    arrays = {name: np.ascontiguousarray(v) for name, v in arrays.items()}
    nc = bacc.Bacc("TRN2", target_bir_lowering=False, num_devices=1, dynamic_dma_scratch_size=1024)
    args = [nc.dram_tensor(name, v.shape, mybir.dt.from_np(v.dtype), kind="ExternalInput").ap()
            for name, v in arrays.items()]
    out = nc.dram_tensor("outT", (D, TOKENS), F32, kind="ExternalOutput").ap()
    adaln_ffn(nc, *args, out)
    result = run_bass_kernel_spmd(nc, [arrays], core_ids=[0])
    outT = np.asarray(result.results[0]["outT"])
    return np.ascontiguousarray(outT.T).reshape(BATCHES, T, D)
```

```python
from contextlib import ExitStack

import concourse.bass as bass
from concourse import mybir

F32 = mybir.dt.float32
F32R = mybir.dt.float32r
BF16 = mybir.dt.bfloat16
I32 = mybir.dt.int32
U32 = mybir.dt.uint32
ALU = mybir.AluOpType
ACT = mybir.ActivationFunctionType
AX_X = mybir.AxisListType.X

P = 128
D = 512
KT = D // P
F = 1376
FT = -(-F // P)
BATCHES, T = 128, 32
SLOTS, R = 32, 16
TOKENS = BATCHES * T
TN = 512
NT = TOKENS // TN
TILE_BATCHES = TN // T
LB = P // R
LN = LB * T
LG = TN // LN
LORA_SCALE = 2.0
NIBBLES = 8
GU_GROUPS = D // P
D_GROUPS = F // P
BANKS = 4
HI, MID, LO = 0, 32, 64
PARTS = 96
Q_SLOTS = 3
EARLY = 6
SP_B = 4
LATE = 10
MEMBER_CUT = FT // 2 * P
D_SLOTS = 2
RES_AT = 4
SPLIT_AT = 7
SPLIT_STEPS = 2
GATHER_AT = 4
GATHER_FIRST = 6
GATHER_SPLIT_AT = 6
LORA_AT = 9


def width(m):
    return min(P, F - m * P)


class BankOrder:

    def __init__(self):
        self.turn, self.fills, self.freed = 0, 0, [0] * BANKS
        self.parts = {}

    def add(self, part, names, repeats=1):
        assert repeats == 1 or len(names) % BANKS == 0
        places, uses, fills = {}, [0] * BANKS, 0
        for n, name in enumerate(names):
            bank = (self.turn + n) % BANKS
            if name is not None:
                fills += 1
                places[name] = (bank, self.fills + fills, self.freed[bank] + uses[bank])
                uses[bank] += 1
        self.parts[part] = (places, fills, uses)
        self.turn += len(names) * repeats
        self.fills += fills * repeats
        self.freed = [a + b * repeats for a, b in zip(self.freed, uses)]

    def bank(self, part, name):
        return self.parts[part][0][name][0]

    def filled(self, part, name, turn=0):
        places, fills, _ = self.parts[part]
        return turn * fills + places[name][1]

    def free(self, part, name, turn=0):
        places, _, uses = self.parts[part]
        bank, _, before = places[name]
        return turn * uses[bank] + before

    def taken(self, part, name, turn=0):
        return self.free(part, name, turn) + 1


def prologue_products():
    zero = [("zero", m, half) for m in range(FT) for half in range(2)]
    return zero[:2 * EARLY] + [("ranks",)] + zero[2 * EARLY:]


def tile_products(grouped, part):
    names = []
    for m in range(FT):
        if part == "first":
            names += [("down zero", m), ("down scale", m)]
        for g in range(GU_GROUPS if grouped else 1):
            names += [("gate", m, g), ("up", m, g)]
        if m == LORA_AT and part != "last":
            names.append(("ranks",))
    if part == "loop":
        names += [None] * (-len(names + KT * [None]) % BANKS)
    if part != "last":
        names += [("cond", j) for j in range(KT)]
    return names


def bank_order(grouped):
    order = BankOrder()
    order.add("prologue", prologue_products())
    if not grouped:
        order.add("weights", [(what, m, half) for m in range(FT) for half in range(2)
                              for what in ("zero", "scale")])
    order.add("first", tile_products(grouped, "first"))
    order.add("loop", tile_products(grouped, "loop"), NT - 2)
    order.add("last", tile_products(grouped, "last"))
    return order


def adaln_ffn(nc, xT, slots, wcT, bias, lora_a, lora_b, q_gu, q_gu_tail, qz_gu, s_gu, s_gu_col,
              s_gu_col_tail, gidx_gu, q_d, qz_d, s_d, gidx_d, outT):
    with ExitStack() as ctx:
        def sb(name, shape, dt=F32):
            return ctx.enter_context(nc.sbuf_tensor(name, shape, dt))

        def sem(name):
            return ctx.enter_context(nc.semaphore(name))

        gu_w = sb("gu_w", [P, FT, 2, KT, P], F32R)
        d_hi = sb("d_hi", [P, FT, D], F32R)
        d_lo = sb("d_lo", [P, FT, D], F32R)
        wc_hi = sb("wc_hi", [P, KT, D], F32R)
        wc_lo = sb("wc_lo", [P, KT, D], F32R)
        x_in = sb("x_in", [P, KT, TN])
        x_hi = sb("x_hi", [P, KT, TN], F32R)
        x_lo = sb("x_lo", [P, KT, TN], F32R)
        res = sb("res", [P, KT, TN])
        y_hi = sb("y_hi", [P, KT, TN], F32R)
        y_lo = sb("y_lo", [P, KT, TN], F32R)
        a_in = sb("a_in", [P, TILE_BATCHES, KT * R])
        a_hi = sb("a_hi", [P, LG, KT, P], F32R)
        a_lo = sb("a_lo", [P, LG, KT, P], F32R)
        b_in = sb("b_in", [P, LG, D])
        b_hi = sb("b_hi", [P, LG, D], F32R)
        b_lo = sb("b_lo", [P, LG, D], F32R)
        mask = sb("mask", [P, LB, T], BF16)
        ranks = sb("ranks", [P, TN])
        ranks_hi = sb("ranks_hi", [P, TN], F32R)
        ranks_lo = sb("ranks_lo", [P, TN], F32R)
        acc = sb("acc", [P, 2, 2, TN])
        h_hi = sb("h_hi", [P, 2, TN], F32R)
        h_lo = sb("h_lo", [P, 2, TN], F32R)
        q_d_sb = sb("q_d_sb", [P, D_SLOTS, D], U32)
        q_gu_sb = sb("q_gu_sb", [P, 2, KT * P], U32)
        w_new = sb("w_new", [P, D_SLOTS, D])
        member = sb("member", [PARTS, D + F], BF16)
        z_gu = sb("z_gu", [GU_GROUPS, 2 * F], BF16)
        z_d = sb("z_d", [D_GROUPS, D], BF16)
        s_d_parts = sb("s_d_parts", [PARTS, D], BF16)
        s_col = sb("s_col", [P, FT, 2, GU_GROUPS])
        bias_sb = sb("bias_sb", [P, KT])
        shift = sb("shift", [P, 1], U32)
        group = sb("group", [P, 1])
        slots_sb = sb("slots_sb", [1, BATCHES], I32)
        qz_d_sb = sb("qz_d_sb", [D_GROUPS, D // NIBBLES], U32)
        odd_rows = sb("odd_rows", [1, 1])
        odd_rows_i = sb("odd_rows_i", [1, 1], I32)
        column = sb("column", [P, 2], I32)

        gidx_sb = res[:].rearrange("p k n -> p (k n)").bitcast(I32)[0:PARTS, 0:D + F]
        gidx_float = gidx_sb.bitcast(F32)
        regular = w_new[0:1, 0, :].bitcast(I32)
        qz_gu_sb = ranks[0:GU_GROUPS, 0:2 * F // NIBBLES].bitcast(U32)
        spare = [acc[:, i // 2, i % 2, :] for i in range(4)]
        z_d_tmp = spare[2].bitcast(U32)[0:D_GROUPS, :]
        scale_in = spare[3][0:PARTS, :]
        scale_rest = spare[2].bitcast(BF16)[0:PARTS, 0:D]
        s_gu_parts = spare[1].bitcast(BF16)[0:PARTS, 0:P]

        ring = ctx.enter_context(nc.psum_tensor("ring", [P, BANKS, TN], F32))
        down_ps = ctx.enter_context(nc.psum_tensor("down_ps", [P, KT, TN], F32))

        wc_in = [(q_gu_sb, q_d_sb)[k // 2][:, k % 2, :].bitcast(F32) for k in range(KT)]
        q_buffers = [buffer.rearrange("p a n -> p (a n)").bitcast(U32)
                     for buffer in (q_gu_sb, w_new, acc[:, 0], q_d_sb)]

        slots_loaded = sem("slots_loaded")
        gidx_gu_loaded = sem("gidx_gu_loaded")
        gidx_d_loaded = sem("gidx_d_loaded")
        qz_gu_loaded = sem("qz_gu_loaded")
        qz_d_loaded = sem("qz_d_loaded")
        s_d_loaded = sem("s_d_loaded")
        columns_loaded = sem("columns_loaded")
        wc_loaded = [sem(f"wc_loaded{k}") for k in range(KT)]
        x0_loaded = [sem(f"x0_loaded{k}") for k in range(KT)]
        x_loaded = sem("x_loaded")
        a_loaded = sem("a_loaded")
        b_loaded = sem("b_loaded")
        q_loaded = [sem(f"q_loaded{i}") for i in range(Q_SLOTS + 1)]
        qd_loaded = [sem(f"qd_loaded{i}") for i in range(D_SLOTS)]
        s_gu_loaded = sem("s_gu_loaded")
        w_moved = sem("w_moved")
        out_stored = sem("out_stored")
        scale_in_cleared = sem("scale_in_cleared")
        indices_made = sem("indices_made")
        constants_made = sem("constants_made")
        pool_step = sem("pool_step")
        mask_made = sem("mask_made")
        dve_step = sem("dve_step")
        member_gu_made = sem("member_gu_made")
        member_d_made = sem("member_d_made")
        form_known = sem("form_known")
        zero_unpacked = sem("zero_unpacked")
        z_gu_made = sem("z_gu_made")
        z_d_made = sem("z_d_made")
        s_d_made = sem("s_d_made")
        s_gu_made = sem("s_gu_made")
        wc_hi_made = sem("wc_hi_made")
        wc_lo_made = sem("wc_lo_made")
        d_hi_made = sem("d_hi_made")
        d_lo_made = sem("d_lo_made")
        x_hi_made = sem("x_hi_made")
        x_lo_made = sem("x_lo_made")
        res_made = sem("res_made")
        adapters_hi_made = sem("adapters_hi_made")
        a_lo_made = sem("a_lo_made")
        b_lo_made = sem("b_lo_made")
        ranks_hi_made = sem("ranks_hi_made")
        ranks_lo_made = sem("ranks_lo_made")
        cond0_filled = sem("cond0_filled")
        y_hi_made = sem("y_hi_made")
        y0_made = sem("y0_made")
        silu_made = sem("silu_made")
        h_made = sem("h_made")
        h_hi_made = sem("h_hi_made")
        h_lo_made = sem("h_lo_made")
        h_used = sem("h_used")
        down_filled = sem("down_filled")
        out_made = sem("out_made")
        filled = sem("filled")
        taken = [sem(f"taken{b}") for b in range(BANKS)]

        orders = {form: bank_order(form) for form in (True, False)}

        def in_both_forms(engine, run):
            engine.wait_ge(form_known, 1)
            odd = engine.value_load(odd_rows_i[0:1, 0:1], min_val=0, max_val=D)
            with engine.If(odd < 1):
                run(True)
            with engine.Else():
                run(False)

        def all_tiles(engine, run):
            run(0, "first", 0)
            with engine.Fori(1, NT - 1) as t:
                run(t, "loop", t - 1)
            run(NT - 1, "last", 0)

        def columns_of(half, m):
            return slice(half * F + m * P, half * F + m * P + width(m))

        def q_place(part, m):
            if part == "prologue":
                return m % Q_SLOTS, m // Q_SLOTS + 1
            slot = m % 2 * Q_SLOTS
            return slot, m // 2 + 1 + (len(range(0, FT, Q_SLOTS)) if slot == 0 else 0)

        def words(part, m):
            return q_buffers[q_place(part, m)[0]][:, 0:2 * KT * width(m)]

        def by_half(q):
            return q.rearrange("p (h k n) -> p h k n", h=2, k=KT)

        def split_of(part, m):
            n, step = KT // SPLIT_STEPS, m - SPLIT_AT
            return range(step * n, (step + 1) * n) if part != "last" and 0 <= step < SPLIT_STEPS else ()

        def slot_of(engine, t, b):
            return engine.value_load(slots_sb[0:1, bass.ds(t * TILE_BATCHES + b, 1)],
                                     min_val=0, max_val=SLOTS - 1)

        def gather_a(engine, b, slot):
            engine.dma_start(a_in[:, b, :], lora_a[bass.ds(slot, 1)].rearrange("o p c -> (o p) c")
                             ).then_inc(a_loaded, 16)

        def gather_b(engine, b, slot):
            engine.dma_start(b_in[b % LB * R:(b % LB + 1) * R, b // LB, :],
                             lora_b[bass.ds(slot, 1)].rearrange("o r n -> (o r) n")
                             ).then_inc(b_loaded, 16)

        def make_member(engine, settle, columns, groups, made):
            idx, wrap = gidx_float[:, columns], member[:, columns]
            settle(engine.tensor_copy(idx, gidx_sb[:, columns]))
            settle(engine.tensor_scalar(wrap, idx, 0.0, float(groups), ALU.is_lt, ALU.mult))
            settle(engine.tensor_tensor(idx, idx, wrap, ALU.add))
            settle(engine.tensor_scalar(idx, idx, 0.0, float(groups - 1), ALU.max, ALU.min))
            engine.tensor_scalar(member[:, columns], idx, group[0:PARTS, 0:1], None,
                                 ALU.is_equal).then_inc(made, 1)

        def side_by_side(ap, m):
            return ap.rearrange("p (k n) -> p k n", n=P)[:, :, 0:width(m)]

        def by_rank(ap):
            return ap.rearrange("p k (b r) -> p k b r", r=R)

        def by_slot(g):
            return a_in[:, g * LB:(g + 1) * LB, :].rearrange("p b (k r) -> p k b r", r=R)

        block = ctx.enter_context(nc.Block())

        @block.sync
        def _(sp):
            def load_x(t):
                sp.wait_ge(res_made, t)
                sp.dma_start(x_in[:], xT[:, bass.ds(t * TN, TN)].rearrange("(k p) n -> p k n", p=P)
                             ).then_inc(x_loaded, 16)

            def gather(t, batches=range(TILE_BATCHES)):
                for b in batches:
                    slot = slot_of(sp, t, b)
                    gather_a(sp, b, slot)
                    gather_b(sp, b, slot)

            def load_q(part, m):
                src = q_gu[m] if m < FT - 1 else q_gu_tail
                sp.dma_start(words(part, m),
                             src.unsqueeze(1).to_broadcast([P // NIBBLES, NIBBLES, src.shape[-1]])
                             ).then_inc(q_loaded[q_place(part, m)[0]], 16)

            def wait_taken(order, part, name):
                sp.wait_ge(taken[order.bank(part, name)], order.taken(part, name))

            def load_q_down(grouped, order, m):
                if m == 0 and not grouped:
                    wait_taken(order, "weights", ("zero", FT - 1, 1))
                if m >= D_SLOTS:
                    wait_taken(order, "first", ("down zero", m - D_SLOTS))
                rows = width(m) // NIBBLES
                src = q_d[m * P // NIBBLES:m * P // NIBBLES + rows, :]
                sp.dma_start(q_d_sb[0:width(m), m % D_SLOTS, :],
                             src.unsqueeze(1).to_broadcast([rows, NIBBLES, D])
                             ).then_inc(qd_loaded[m % D_SLOTS], 16)

            sp.dma_start(slots_sb[:], slots).then_inc(slots_loaded, 16)
            sp.dma_start(gidx_sb[:, 0:D], gidx_gu.to_broadcast([PARTS, D])).then_inc(gidx_gu_loaded, 16)
            for k in range(KT):
                sp.dma_start(x_in[:, k, :], xT[k * P:(k + 1) * P, 0:TN]).then_inc(x0_loaded[k], 16)
                sp.dma_start(wc_in[k], wcT[k * P:(k + 1) * P, :]).then_inc(wc_loaded[k], 16)
                if k == 0:
                    sp.dma_start(qz_gu_sb, qz_gu).then_inc(qz_gu_loaded, 16)
            sp.dma_start(gidx_sb[:, D:D + F], gidx_d.to_broadcast([PARTS, F])).then_inc(gidx_d_loaded, 16)

            sp.dma_start(qz_d_sb[:], qz_d).then_inc(qz_d_loaded, 16)
            sp.wait_ge(scale_in_cleared, 1)

            sp.wait_ge(slots_loaded, 16)
            batches = iter(range(TILE_BATCHES))
            for m, between in enumerate((3, 1, 6, 3, 2, 1)):
                for _ in range(between):
                    b = next(batches)
                    gather_a(sp, b, slot_of(sp, 0, b))
                if m == 0:
                    sp.wait_ge(wc_lo_made, 2)
                elif m == 1:
                    sp.wait_ge(form_known, 1)
                elif m == 2:
                    sp.wait_ge(z_gu_made, NIBBLES)
                else:
                    wait_taken(orders[True], "prologue", ("zero", m - Q_SLOTS, 1))
                load_q("prologue", m)
            for m in range(EARLY, FT):
                b = TILE_BATCHES - SP_B + m - EARLY
                if b < TILE_BATCHES:
                    gather_b(sp, b, slot_of(sp, 0, b))
                if m == EARLY:
                    for part in (HI, MID, LO):
                        sp.dma_start(scale_in[part:part + D_GROUPS, :], s_d).then_inc(s_d_loaded, 16)
                    sp.dma_start(bias_sb[:], bias).then_inc(columns_loaded, 16)
                wait_taken(orders[True], "prologue", ("zero", m - Q_SLOTS, 1))
                load_q("prologue", m)
            sp.dma_start(s_col[:, 0:FT - 1, :, :], s_gu_col).then_inc(columns_loaded, 16)
            sp.dma_start(s_col[0:width(FT - 1), FT - 1, :, :], s_gu_col_tail).then_inc(columns_loaded, 16)

            def tiles(grouped):
                order = orders[grouped]

                if not grouped:
                    for m in range(FT):
                        if m == 0:
                            wait_taken(order, "prologue", ("zero", (FT - 1) // Q_SLOTS * Q_SLOTS, 1))
                        elif m >= 2:
                            wait_taken(order, "weights", ("zero", m - 2, 1))
                        load_q("weights", m)
                        for half in range(2):
                            i = 2 * m + half
                            if i == 0:
                                sp.wait_ge(s_d_made, 1)
                            else:
                                sp.wait_ge(s_gu_made, i)
                            for part in (HI, MID, LO):
                                sp.dma_start(scale_in[part:part + GU_GROUPS, 0:width(m)],
                                             s_gu[:, columns_of(half, m)]).then_inc(s_gu_loaded, 16)
                            wait_taken(order, "weights", ("scale", m, half))
                            sp.dma_start(gu_w[:, m, half, :, 0:width(m)].bitcast(F32),
                                         w_new[:, 0, 0:KT * width(m)].rearrange(
                                             "p (k n) -> p k n", k=KT)).then_inc(w_moved, 16)

                def store(t):
                    for j in range(KT):
                        sp.wait_ge(out_made, KT * t + j + 1)
                        sp.dma_start(outT[j * P:(j + 1) * P, bass.ds(t * TN, TN)],
                                     res[:, j, :]).then_inc(out_stored, 16)

                def tile(t, part, turn):
                    if part == "first":
                        for m in range(FT):
                            load_q_down(grouped, order, m)
                            if m == 0:
                                sp.wait_ge(a_lo_made, LG)
                                sp.wait_ge(b_lo_made, 1)
                            if m * GATHER_AT < TILE_BATCHES:
                                gather(1, range(m * GATHER_AT, (m + 1) * GATHER_AT))
                            if m == RES_AT + D_SLOTS:
                                load_x(1)
                    else:
                        if part == "loop":
                            sp.wait_ge(a_lo_made, LG * (t + 1))
                            sp.wait_ge(b_lo_made, t + 1)
                            gather(t + 1, range(GATHER_FIRST))
                        store(t - 1)
                        if part == "loop":
                            gather(t + 1, range(GATHER_FIRST, TILE_BATCHES))
                            load_x(t + 1)
                    if part == "last":
                        store(t)

                all_tiles(sp, tile)
                sp.wait_ge(out_stored, 16 * KT * NT)

            in_both_forms(sp, tiles)

        @block.gpsimd
        def _(pool):
            pool.memset(scale_in, 0.0).then_inc(scale_in_cleared, 1)
            pool.iota(column[:, 0:1], [[0, 1]], base=0, channel_multiplier=1)
            pool.iota(column[:, 1:2], [[0, 1]], base=0, channel_multiplier=4)
            pool.iota(regular.rearrange("o (k p) -> o k p", p=P), [[1, KT], [0, P]], base=0,
                      channel_multiplier=0).then_inc(indices_made, 1)
            pool.memset(mask[:], LORA_SCALE).then_inc(mask_made, 1)
            pool.wait_ge(mask_made, 1)
            pool.affine_select(out=mask[:], in_=mask[:], compare_op=ALU.is_ge, fill=0.0, base=0,
                               pattern=[[-R, LB], [0, T]], channel_multiplier=1).then_inc(mask_made, 1)
            pool.wait_ge(mask_made, 2)
            pool.affine_select(out=mask[:], in_=mask[:], compare_op=ALU.is_ge, fill=0.0, base=R - 1,
                               pattern=[[R, LB], [0, T]], channel_multiplier=-1).then_inc(mask_made, 1)

            steps = [0]

            def settle(instruction):
                steps[0] += 1
                instruction.then_inc(pool_step, 1)
                pool.wait_ge(pool_step, steps[0])

            pool.wait_ge(constants_made, 1)
            pool.wait_ge(gidx_d_loaded, 16)
            make_member(pool, settle, slice(D, D + MEMBER_CUT), D_GROUPS, member_d_made)

            def a_low(t):
                for g in range(LG):
                    pool.wait_ge(adapters_hi_made, (LG + 1) * t + g + 1)
                    pool.tensor_tensor(by_rank(a_lo[:, g]), by_slot(g), by_rank(a_hi[:, g].bitcast(F32)),
                                       ALU.subtract).then_inc(a_lo_made, 1)

            def b_low(t):
                pool.wait_ge(adapters_hi_made, (LG + 1) * (t + 1))
                pool.tensor_tensor(b_lo[:], b_in[:], b_hi[:].bitcast(F32),
                                   ALU.subtract).then_inc(b_lo_made, 1)

            def ranks_low(t):
                pool.wait_ge(ranks_hi_made, t + 1)
                pool.tensor_tensor(ranks_lo[:], ranks[:], ranks_hi[:].bitcast(F32),
                                   ALU.subtract).then_inc(ranks_lo_made, 1)

            a_low(0)
            ranks_low(0)
            make_member(pool, settle, slice(D + MEMBER_CUT, D + F), D_GROUPS, member_d_made)

            def tiles(grouped):
                order = orders[grouped]

                def product(t, part, turn, m):
                    a = acc[0:width(m), m % 2]
                    name = ("up", m, GU_GROUPS - 1)
                    pool.wait_ge(silu_made, FT * t + m + 1)
                    pool.wait_ge(taken[order.bank(part, name)], order.taken(part, name, turn))
                    pool.tensor_tensor(a[:, 1], a[:, 0], a[:, 1], ALU.mult).then_inc(h_made, 1)

                def h_low(t, m):
                    n = width(m)
                    pool.wait_ge(h_hi_made, FT * t + m + 1)
                    pool.tensor_tensor(h_lo[0:n, m % 2], acc[0:n, m % 2, 1], h_hi[0:n, m % 2].bitcast(F32),
                                       ALU.subtract).then_inc(h_lo_made, 1)

                def tile(t, part, turn):
                    for m in range(FT):
                        if m >= 1:
                            h_low(t, m - 1)
                        if part == "first":
                            n = width(m)
                            pool.wait_ge(d_hi_made, m + 1)
                            pool.tensor_tensor(d_lo[0:n, m], w_new[0:n, m % D_SLOTS], d_hi[0:n, m].bitcast(F32),
                                               ALU.subtract).then_inc(d_lo_made, 1)
                        if part != "last" and m == GATHER_SPLIT_AT:
                            a_low(t + 1)
                            b_low(t + 1)
                        if grouped:
                            product(t, part, turn, m)
                        if part != "last" and m == LORA_AT:
                            ranks_low(t + 1)
                    h_low(t, FT - 1)

                all_tiles(pool, tile)

            in_both_forms(pool, tiles)

        @block.scalar
        def _(act):
            def a_high(t):
                act.wait_ge(a_loaded, 16 * TILE_BATCHES * (t + 1))
                for g in range(LG):
                    act.activation(by_rank(a_hi[:, g]), by_slot(g), ACT.Copy).then_inc(adapters_hi_made, 1)

            def b_high(t):
                act.wait_ge(b_loaded, 16 * TILE_BATCHES * (t + 1))
                act.activation(b_hi[:], b_in[:], ACT.Copy).then_inc(adapters_hi_made, 1)

            def ranks_high(order, part, turn, t):
                bank = order.bank(part, ("ranks",))
                act.wait_ge(taken[bank], order.taken(part, ("ranks",), turn))
                act.activation(ranks_hi[:], ranks[:], ACT.Copy).then_inc(ranks_hi_made, 1)

            def round_y(j, product):
                act.activation(y_hi[:, j, :], product, ACT.Identity,
                               bias=bias_sb[:, j:j + 1]).then_inc(y_hi_made, 1)

            def cond_high(order, part, turn, j):
                act.wait_ge(filled, order.filled(part, ("cond", j), turn))
                round_y(j, ring[:, order.bank(part, ("cond", j)), :])

            for k in range(KT):
                act.wait_ge(x0_loaded[k], 16)
                act.activation(x_hi[:, k, :], x_in[:, k, :], ACT.Copy).then_inc(x_hi_made, 1)
                act.wait_ge(wc_loaded[k], 16)
                act.activation(wc_hi[:, k, :], wc_in[k], ACT.Copy).then_inc(wc_hi_made, 1)
            for n in range(NIBBLES):
                act.wait_ge(zero_unpacked, n + 1)
                act.activation(z_gu[:, n:2 * F:NIBBLES],
                               spare[n % 3].bitcast(U32)[0:GU_GROUPS, 0:2 * F // NIBBLES],
                               ACT.Copy, bias=1.0).then_inc(z_gu_made, 1)
            act.wait_ge(slots_loaded, 16)
            for b in range(TILE_BATCHES - SP_B):
                if b == LB:
                    a_high(0)
                gather_b(act, b, slot_of(act, 0, b))
            b_high(0)
            ranks_high(orders[True], "prologue", 0, 0)
            act.wait_ge(columns_loaded, 48)
            for j in range(KT):
                act.wait_ge(cond0_filled, j + 1)
                round_y(j, down_ps[:, j, :])

            def tiles(grouped):
                order = orders[grouped]

                def start_group(t, part, turn, m, half):
                    name = (("gate", "up")[half], m, 0)
                    bank, n = order.bank(part, name), width(m)
                    act.wait_ge(filled, order.filled(part, name, turn))
                    act.activation(acc[0:n, m % 2, half], ring[0:n, bank, :], ACT.Copy,
                                   scale=s_col[0:n, m, half, 0:1]).then_inc(taken[bank], 1)

                def acc_free(t, part, m):
                    if m >= 2:
                        act.wait_ge(h_lo_made, FT * t + m - 1)
                    elif part != "first":
                        act.wait_ge(h_lo_made, FT * t)

                def silu(t, part, turn, m):
                    a = acc[0:width(m), m % 2, 0]
                    if grouped:
                        name = ("gate", m, GU_GROUPS - 1)
                        act.wait_ge(taken[order.bank(part, name)], order.taken(part, name, turn))
                        act.activation(a, a, ACT.Silu).then_inc(silu_made, 1)
                    else:
                        name = ("gate", m, 0)
                        bank = order.bank(part, name)
                        act.wait_ge(filled, order.filled(part, name, turn))
                        act.activation(a, ring[0:width(m), bank, :], ACT.Silu).then_inc(taken[bank], 1)

                def h_high(t, part, turn, m):
                    n = width(m)
                    if grouped:
                        act.wait_ge(h_made, FT * t + m + 1)
                    else:
                        name = ("up", m, 0)
                        act.wait_ge(taken[order.bank(part, name)], order.taken(part, name, turn))
                    if m >= 2:
                        act.wait_ge(h_used, (FT - 1) * t + m - 1)
                    elif part != "first":
                        if m == 0:
                            act.wait_ge(h_used, (FT - 1) * t)
                        else:
                            act.wait_ge(down_filled, KT * t)
                    act.activation(h_hi[0:n, m % 2], acc[0:n, m % 2, 1], ACT.Copy).then_inc(h_hi_made, 1)

                def copy_residual(t, part):
                    act.wait_ge(x_lo_made, KT * (t + 1))
                    if part == "first":
                        act.wait_ge(member_d_made, 2)
                    else:
                        act.wait_ge(out_stored, 16 * KT * t)
                    for k in range(KT):
                        c = act.activation(res[:, k, :], x_in[:, k, :], ACT.Copy)
                    c.then_inc(res_made, 1)

                def tile(t, part, turn):
                    for m in range(FT):
                        acc_free(t, part, m)
                        if grouped:
                            for half in range(2):
                                start_group(t, part, turn, m, half)
                        if m >= 1:
                            h_high(t, part, turn, m - 1)
                        if part == "first":
                            n, name = width(m), ("down scale", m)
                            act.wait_ge(taken[order.bank(part, name)], order.taken(part, name))
                            act.activation(d_hi[0:n, m], w_new[0:n, m % D_SLOTS], ACT.Copy).then_inc(d_hi_made, 1)
                        if m == RES_AT:
                            copy_residual(t, part)
                        for k in split_of(part, m):
                            act.wait_ge(x_loaded, 16 * (t + 1))
                            act.activation(x_hi[:, k, :], x_in[:, k, :], ACT.Copy).then_inc(x_hi_made, 1)
                        if part != "last" and m == GATHER_SPLIT_AT:
                            a_high(t + 1)
                            b_high(t + 1)
                        silu(t, part, turn, m)
                        if part != "last" and m == LORA_AT:
                            ranks_high(order, part, turn, t + 1)
                    h_high(t, part, turn, FT - 1)
                    if part != "last":
                        for j in range(KT):
                            cond_high(order, part, turn, j)

                all_tiles(act, tile)

            in_both_forms(act, tiles)

        @block.vector
        def _(dve):
            steps = [0]

            def settle(instruction):
                steps[0] += 1
                instruction.then_inc(dve_step, 1)
                dve.wait_ge(dve_step, steps[0])

            def split_scale(parts, made):
                n = parts.shape[-1]
                rest, s = scale_rest[:, 0:n], scale_in[:, 0:n]
                settle(dve.tensor_copy(parts, s))
                settle(dve.tensor_tensor(s, s, parts, ALU.subtract))
                settle(dve.tensor_copy(rest, s))
                settle(dve.tensor_copy(parts[MID:LO], rest[MID:LO]))
                settle(dve.tensor_tensor(s, s, rest, ALU.subtract))
                dve.tensor_copy(parts[LO:PARTS], s[LO:PARTS]).then_inc(made, 1)

            def unpack(q):
                settle(dve.tensor_scalar(q, q, shift[0:q.shape[0], 0:1], 15,
                                         ALU.logical_shift_right, ALU.bitwise_and))

            def x_low(k):
                dve.tensor_tensor(x_lo[:, k, :], x_in[:, k, :], x_hi[:, k, :].bitcast(F32),
                                  ALU.subtract).then_inc(x_lo_made, 1)

            def unpack_gate_up(part, m):
                slot, loads = q_place(part, m)
                dve.wait_ge(q_loaded[slot], 16 * loads)
                unpack(words(part, m))

            def zero_weights(m):
                order, part = orders[True], "prologue"
                unpack_gate_up(part, m)
                for half in range(2):
                    bank = order.bank(part, ("zero", m, half))
                    dve.wait_ge(filled, order.filled(part, ("zero", m, half)))
                    dve.tensor_tensor(gu_w[:, m, half, :, 0:width(m)], by_half(words(part, m))[:, half],
                                      side_by_side(ring[:, bank, :], m),
                                      ALU.subtract).then_inc(taken[bank], 1)

            def take_ranks(order, part, turn, t):
                bank = order.bank(part, ("ranks",))
                if part != "prologue":
                    dve.wait_ge(ranks_lo_made, t)
                dve.wait_ge(filled, order.filled(part, ("ranks",), turn))
                for g in range(LG):
                    r = dve.tensor_tensor(ranks[:, g * LN:(g + 1) * LN], ring[:, bank, g * LN:(g + 1) * LN],
                                          mask[:].rearrange("p b t -> p (b t)"), ALU.mult)
                r.then_inc(taken[bank], 1)

            def y_rest(t, j, product):
                dve.wait_ge(y_hi_made, KT * t + j + 1)
                return dve.scalar_tensor_tensor(y_lo[:, j, :], product, bias_sb[:, j:j + 1],
                                                y_hi[:, j, :].bitcast(F32), ALU.add, ALU.subtract)

            def cond_low(order, part, turn, t, j):
                bank = order.bank(part, ("cond", j))
                y_rest(t, j, ring[:, bank, :]).then_inc(taken[bank], 1)

            dve.wait_ge(indices_made, 1)
            settle(dve.tensor_scalar(column[:, 0:1], column[:, 0:1], 31, None, ALU.bitwise_and))
            dve.tensor_copy(group[:], column[:, 0:1])
            dve.tensor_scalar(shift[:], column[:, 1:2].bitcast(U32), 4 * (NIBBLES - 1), None,
                              ALU.bitwise_and).then_inc(constants_made, 1)
            dve.wait_ge(constants_made, 1)
            dve.wait_ge(gidx_gu_loaded, 16)
            make_member(dve, settle, slice(0, D), GU_GROUPS, member_gu_made)
            dve.wait_ge(member_gu_made, 1)
            odd = gidx_float[0:1, 0:D]
            settle(dve.tensor_tensor(odd, odd, regular, ALU.not_equal))
            settle(dve.reduce_sum(odd_rows[:], odd, axis=AX_X))
            dve.tensor_copy(odd_rows_i[:], odd_rows[:]).then_inc(form_known, 1)

            for k in range(KT):
                dve.wait_ge(x_hi_made, k + 1)
                x_low(k)
                dve.wait_ge(wc_hi_made, k + 1)
                dve.tensor_tensor(wc_lo[:, k, :], wc_in[k], wc_hi[:, k, :].bitcast(F32),
                                  ALU.subtract).then_inc(wc_lo_made, 1)

            dve.wait_ge(qz_gu_loaded, 16)
            for n in range(NIBBLES):
                if n >= 3:
                    dve.wait_ge(z_gu_made, n - 2)
                dve.tensor_scalar(spare[n % 3].bitcast(U32)[0:GU_GROUPS, 0:2 * F // NIBBLES],
                                  qz_gu_sb, 4 * n, 15, ALU.logical_shift_right,
                                  ALU.bitwise_and).then_inc(zero_unpacked, 1)
            dve.wait_ge(z_gu_made, NIBBLES)

            for m in range(EARLY):
                zero_weights(m)
            dve.wait_ge(qz_d_loaded, 16)
            z_columns = z_d_tmp.rearrange("g (c n) -> g c n", n=NIBBLES)
            for n in range(NIBBLES):
                z = dve.tensor_scalar(z_columns[:, :, n], qz_d_sb[:], 4 * n, 15, ALU.logical_shift_right,
                                      ALU.bitwise_and)
            settle(z)
            dve.tensor_scalar(z_d[:], z_d_tmp, 1.0, None, ALU.add).then_inc(z_d_made, 1)
            dve.wait_ge(z_d_made, 1)
            dve.wait_ge(s_d_loaded, 48)
            split_scale(s_d_parts[:], s_d_made)
            dve.wait_ge(mask_made, 3)
            take_ranks(orders[True], "prologue", 0, 0)
            zero_weights(EARLY)
            dve.wait_ge(adapters_hi_made, LG + 1)
            dve.tensor_tensor(b_lo[:], b_in[:], b_hi[:].bitcast(F32), ALU.subtract).then_inc(b_lo_made, 1)
            for m in range(EARLY + 1, LATE):
                zero_weights(m)
            dve.wait_ge(columns_loaded, 48)
            for j in range(KT):
                y_rest(0, j, down_ps[:, j, :]).then_inc(y0_made, 1)
            for m in range(LATE, FT):
                zero_weights(m)
            before_forms = steps[0]

            def tiles(grouped):
                order = orders[grouped]
                steps[0] = before_forms

                if not grouped:
                    for m in range(FT):
                        n = width(m)
                        unpack_gate_up("weights", m)
                        for half in range(2):
                            i = 2 * m + half
                            dve.wait_ge(s_gu_loaded, 48 * (i + 1))
                            split_scale(s_gu_parts[:, 0:n], s_gu_made)
                            if i >= 1:
                                dve.wait_ge(w_moved, 16 * i)
                            w = w_new[:, 0, 0:KT * n].rearrange("p (k n) -> p k n", k=KT)
                            zero = order.bank("weights", ("zero", m, half))
                            dve.wait_ge(filled, order.filled("weights", ("zero", m, half)))
                            dve.tensor_tensor(w, by_half(words("weights", m))[:, half],
                                              side_by_side(ring[:, zero, :], m),
                                              ALU.subtract).then_inc(taken[zero], 1)
                            scale = order.bank("weights", ("scale", m, half))
                            dve.wait_ge(taken[zero], order.taken("weights", ("zero", m, half)))
                            dve.wait_ge(filled, order.filled("weights", ("scale", m, half)))
                            dve.tensor_tensor(w, w, side_by_side(ring[:, scale, :], m),
                                              ALU.mult).then_inc(taken[scale], 1)

                def down_weights(m):
                    n = width(m)
                    zero, scale = [order.bank("first", (what, m)) for what in ("down zero", "down scale")]
                    q, w = q_d_sb[0:n, m % D_SLOTS], w_new[0:n, m % D_SLOTS]
                    dve.wait_ge(qd_loaded[m % D_SLOTS], 16 * (m // D_SLOTS + 1))
                    unpack(q)
                    if m >= D_SLOTS:
                        dve.wait_ge(d_lo_made, m - D_SLOTS + 1)
                    elif m == 0 and not grouped:
                        dve.wait_ge(w_moved, 16 * 2 * FT)
                    dve.wait_ge(filled, order.filled("first", ("down zero", m)))
                    dve.tensor_tensor(w, q, ring[0:n, zero, :], ALU.subtract).then_inc(taken[zero], 1)
                    dve.wait_ge(taken[zero], order.taken("first", ("down zero", m)))
                    dve.wait_ge(filled, order.filled("first", ("down scale", m)))
                    dve.tensor_tensor(w, w, ring[0:n, scale, :], ALU.mult).then_inc(taken[scale], 1)

                def add_group(part, turn, m, half, g):
                    what, n = ("gate", "up")[half], width(m)
                    bank, last = order.bank(part, (what, m, g)), order.bank(part, (what, m, g - 1))
                    a = acc[0:n, m % 2, half]
                    dve.wait_ge(taken[last], order.taken(part, (what, m, g - 1), turn))
                    dve.wait_ge(filled, order.filled(part, (what, m, g), turn))
                    dve.scalar_tensor_tensor(a, ring[0:n, bank, :], s_col[0:n, m, half, g:g + 1], a,
                                             ALU.mult, ALU.add).then_inc(taken[bank], 1)

                def product(part, turn, m):
                    n = width(m)
                    gate, up = [order.bank(part, (what, m, 0)) for what in ("gate", "up")]
                    dve.wait_ge(taken[gate], order.taken(part, ("gate", m, 0), turn))
                    dve.wait_ge(filled, order.filled(part, ("up", m, 0), turn))
                    dve.tensor_tensor(acc[0:n, m % 2, 1], acc[0:n, m % 2, 0], ring[0:n, up, :],
                                      ALU.mult).then_inc(taken[up], 1)

                def output(t, j):
                    if j == 0:
                        dve.wait_ge(res_made, t + 1)
                    dve.wait_ge(down_filled, KT * t + j + 1)
                    dve.tensor_tensor(res[:, j, :], res[:, j, :], down_ps[:, j, :],
                                      ALU.add).then_inc(out_made, 1)

                def tile(t, part, turn):
                    for m in range(FT):
                        if part == "first":
                            down_weights(m)
                        if grouped:
                            for g in range(1, GU_GROUPS):
                                for half in range(2):
                                    add_group(part, turn, m, half, g)
                                j = (m - 1) * (GU_GROUPS - 1) + g - 1
                                if part != "first" and m >= 1 and j < KT:
                                    output(t - 1, j)
                        else:
                            product(part, turn, m)
                            if part != "first" and m == 1:
                                for j in range(KT):
                                    output(t - 1, j)
                        for k in split_of(part, m):
                            dve.wait_ge(x_hi_made, KT * (t + 1) + k + 1)
                            x_low(k)
                        if part != "last" and m == LORA_AT:
                            take_ranks(order, part, turn, t + 1)
                    if part != "last":
                        for j in range(KT):
                            cond_low(order, part, turn, t + 1, j)
                    else:
                        for j in range(KT):
                            output(t, j)

                all_tiles(dve, tile)

            in_both_forms(dve, tiles)

        @block.tensor
        def _(pe):
            def wait_free(order, part, name, turn=0):
                bank, before = order.bank(part, name), order.free(part, name, turn)
                if not (isinstance(before, int) and before == 0):
                    pe.wait_ge(taken[bank], before)
                return bank

            def split_product(out, w_hi, w_lo, v_hi, v_lo, start, stop):
                pe.matmul(out, w_hi, v_hi, start=start, stop=False)
                pe.matmul(out, w_hi, v_lo, start=False, stop=False)
                return pe.matmul(out, w_lo, v_hi, start=False, stop=stop)

            def ranks_product(order, part, turn, t):
                bank = wait_free(order, part, ("ranks",), turn)
                pe.wait_ge(x_lo_made, KT * (t + 1))
                for g in range(LG):
                    pe.wait_ge(a_lo_made, LG * t + g + 1)
                    tokens = slice(g * LN, (g + 1) * LN)
                    for k in range(KT):
                        mm = split_product(ring[:, bank, tokens], a_hi[:, g, k], a_lo[:, g, k],
                                           x_hi[:, k, tokens], x_lo[:, k, tokens], k == 0, k == KT - 1)
                mm.then_inc(filled, 1)

            def adapter_product(out, j):
                columns = slice(j * P, (j + 1) * P)
                for g in range(LG):
                    tokens = slice(g * LN, (g + 1) * LN)
                    split_product(out[:, tokens], b_hi[:, g, columns], b_lo[:, g, columns],
                                  ranks_hi[:, tokens], ranks_lo[:, tokens], False, False)

            def cond_product(order, part, turn, t, j):
                bank = wait_free(order, part, ("cond", j), turn)
                columns = slice(j * P, (j + 1) * P)
                if j == 0:
                    pe.wait_ge(ranks_lo_made, t + 1)
                    pe.wait_ge(b_lo_made, t + 1)
                for k in range(KT):
                    mm = split_product(ring[:, bank, :], wc_hi[:, k, columns], wc_lo[:, k, columns],
                                       x_hi[:, k, :], x_lo[:, k, :], k == 0, k == KT - 1)
                    if k == 0:
                        adapter_product(ring[:, bank, :], j)
                mm.then_inc(filled, 1)

            def zero_product(order, part, m, half):
                bank = wait_free(order, part, ("zero", m, half))
                for k in range(KT):
                    mm = pe.matmul(ring[:, bank, k * P:k * P + width(m)],
                                   member[0:GU_GROUPS, k * P:(k + 1) * P], z_gu[:, columns_of(half, m)],
                                   start=True, stop=True)
                mm.then_inc(filled, 1)

            def wc_lo_product(j, k, stop):
                return pe.matmul(down_ps[:, j, :], wc_lo[:, k, j * P:(j + 1) * P], x_hi[:, k, :],
                                 start=False, stop=stop)

            for k in range(KT):
                if k == KT - 1:
                    pe.wait_ge(member_gu_made, 1)
                    pe.wait_ge(z_gu_made, NIBBLES)
                    for m in range(2):
                        for half in range(2):
                            zero_product(orders[True], "prologue", m, half)
                pe.wait_ge(wc_lo_made, k + 1)
                for j in range(KT):
                    w = wc_hi[:, k, j * P:(j + 1) * P]
                    pe.matmul(down_ps[:, j, :], w, x_hi[:, k, :], start=(k == 0), stop=False)
                    pe.matmul(down_ps[:, j, :], w, x_lo[:, k, :], start=False, stop=False)
                    if k < KT - 1:
                        wc_lo_product(j, k, False)
            for m in range(2, EARLY):
                for half in range(2):
                    zero_product(orders[True], "prologue", m, half)
            ranks_product(orders[True], "prologue", 0, 0)
            for m in range(EARLY, LATE):
                for half in range(2):
                    zero_product(orders[True], "prologue", m, half)
            pe.wait_ge(ranks_lo_made, 1)
            pe.wait_ge(b_lo_made, 1)
            for j in range(KT):
                adapter_product(down_ps[:, j, :], j)
                wc_lo_product(j, KT - 1, True).then_inc(cond0_filled, 1)
            for m in range(LATE, FT):
                for half in range(2):
                    zero_product(orders[True], "prologue", m, half)

            def tiles(grouped):
                order = orders[grouped]
                pe.wait_ge(y0_made, KT)

                if not grouped:
                    for m in range(FT):
                        for half in range(2):
                            zero_product(order, "weights", m, half)
                            bank = wait_free(order, "weights", ("scale", m, half))
                            pe.wait_ge(s_gu_made, 2 * m + half + 1)
                            for k in range(KT):
                                mm = pe.matmul(ring[:, bank, k * P:k * P + width(m)],
                                               member[:, k * P:(k + 1) * P], s_gu_parts[:, 0:width(m)],
                                               start=True, stop=True)
                            mm.then_inc(filled, 1)
                    pe.wait_ge(w_moved, 16 * 2 * FT)

                def down_weight_products(m):
                    rows = slice(D + m * P, D + m * P + width(m))
                    bank = wait_free(order, "first", ("down zero", m))
                    if m == 0:
                        pe.wait_ge(member_d_made, 1)
                        pe.wait_ge(s_d_made, 1)
                    elif m * P == MEMBER_CUT:
                        pe.wait_ge(member_d_made, 2)
                    pe.matmul(ring[0:width(m), bank, :], member[0:D_GROUPS, rows], z_d[:],
                              start=True, stop=True).then_inc(filled, 1)
                    bank = wait_free(order, "first", ("down scale", m))
                    pe.matmul(ring[0:width(m), bank, :], member[:, rows], s_d_parts[:],
                              start=True, stop=True).then_inc(filled, 1)

                def group_product(part, turn, m, half, g):
                    name, n = (("gate", "up")[half], m, g), width(m)
                    bank = wait_free(order, part, name, turn)
                    w = gu_w[:, m, half, g, 0:n]
                    pe.matmul(ring[0:n, bank, :], w, y_hi[:, g, :], start=True, stop=False)
                    pe.matmul(ring[0:n, bank, :], w, y_lo[:, g, :], start=False,
                              stop=True).then_inc(filled, 1)

                def general_product(part, turn, m, half):
                    name, n = (("gate", "up")[half], m, 0), width(m)
                    bank = wait_free(order, part, name, turn)
                    for k in range(KT):
                        w = gu_w[:, m, half, k, 0:n].bitcast(F32)
                        pe.matmul(ring[0:n, bank, :], w, y_hi[:, k, :].bitcast(F32),
                                  start=(k == 0), stop=False)
                        mm = pe.matmul(ring[0:n, bank, :], w, y_lo[:, k, :].bitcast(F32),
                                       start=False, stop=(k == KT - 1))
                    mm.then_inc(filled, 1)

                def down_product(t, part, m, js):
                    n = width(m)
                    final = m == (FT - 1 if part == "last" else FT - 2)
                    if js[0] == 0:
                        pe.wait_ge(h_lo_made, FT * t + m + 1)
                        if part == "first":
                            pe.wait_ge(d_lo_made, m + 1)
                    for j in js:
                        columns = slice(j * P, (j + 1) * P)
                        if m == 0 and part != "first":
                            pe.wait_ge(out_made, KT * (t - 1) + j + 1)
                        mm = split_product(down_ps[:, j, :], d_hi[0:n, m, columns], d_lo[0:n, m, columns],
                                           h_hi[0:n, m % 2], h_lo[0:n, m % 2], m == 0, final)
                        if final:
                            mm.then_inc(down_filled, 1)
                    if not final and js[-1] == KT - 1:
                        mm.then_inc(h_used, 1)

                def down_products(t, part, m, js):
                    if m >= 2:
                        down_product(t, part, m - 2, js)
                    elif part == "loop" or part == "last":
                        down_product(t - 1, "loop", FT - 1 - m, js)

                def tile(t, part, turn):
                    for m in range(FT):
                        if part == "first":
                            down_weight_products(m)
                            if grouped:
                                for half in range(2):
                                    name = ("zero", m, half)
                                    pe.wait_ge(taken[order.bank("prologue", name)],
                                               order.taken("prologue", name))
                        if grouped:
                            for g in range(GU_GROUPS):
                                for half in range(2):
                                    group_product(part, turn, m, half, g)
                                down_products(t, part, m, [g])
                        else:
                            for half in range(2):
                                general_product(part, turn, m, half)
                            down_products(t, part, m, range(KT))
                        if part != "last" and m == LORA_AT:
                            ranks_product(order, part, turn, t + 1)
                    if part != "last":
                        for j in range(KT):
                            cond_product(order, part, turn, t + 1, j)
                        if part == "first":
                            pe.wait_ge(d_lo_made, FT)
                        if not grouped:
                            for j in range(KT):
                                name = ("cond", j)
                                pe.wait_ge(taken[order.bank(part, name)], order.taken(part, name, turn))
                    else:
                        for m in (FT - 2, FT - 1):
                            down_product(t, part, m, range(KT))

                all_tiles(pe, tile)

            in_both_forms(pe, tiles)


def kernel(**inputs):
    import numpy as np
    import concourse.bacc as bacc
    from concourse.bass_utils import run_bass_kernel_spmd

    a = {name: np.asarray(v) for name, v in inputs.items()}
    full = (FT - 1) * P
    q_gu = a["L0_ffn_qweight_gu"].reshape(KT, P // NIBBLES, 2, F).transpose(1, 2, 0, 3)
    s_gu = a["L0_ffn_scales_gu"].reshape(GU_GROUPS, 2, F)
    arrays = {
        "xT": a["x"].reshape(TOKENS, D).T,
        "slots": a["itok_B_0_23"].reshape(1, BATCHES),
        "wcT": a["L0_cond_W"].T,
        "bias": a["L0_cond_b"].reshape(KT, P).T,
        "lora_a": a["L0_cond_lora_As"].reshape(SLOTS, KT, P, R).transpose(0, 2, 1, 3).reshape(
            SLOTS, P, KT * R),
        "lora_b": a["L0_cond_lora_Bs"],
        "q_gu": q_gu[..., :full].reshape(P // NIBBLES, 2, KT, FT - 1, P).transpose(3, 0, 1, 2, 4).reshape(
            FT - 1, P // NIBBLES, 2 * KT * P),
        "q_gu_tail": q_gu[..., full:].reshape(P // NIBBLES, -1),
        "qz_gu": a["L0_ffn_qzeros_gu"],
        "s_gu": a["L0_ffn_scales_gu"],
        "s_gu_col": s_gu[..., :full].reshape(GU_GROUPS, 2, FT - 1, P).transpose(3, 2, 1, 0),
        "s_gu_col_tail": s_gu[..., full:].transpose(2, 1, 0),
        "gidx_gu": a["L0_ffn_g_idx_gu"].reshape(1, D),
        "q_d": a["L0_ffn_qweight_down"],
        "qz_d": a["L0_ffn_qzeros_down"],
        "s_d": a["L0_ffn_scales_down"],
        "gidx_d": a["L0_ffn_g_idx_down"].reshape(1, F),
    }
    arrays = {name: np.ascontiguousarray(v) for name, v in arrays.items()}
    nc = bacc.Bacc("TRN2", target_bir_lowering=False, num_devices=1, dynamic_dma_scratch_size=1024)
    args = [nc.dram_tensor(name, v.shape, mybir.dt.from_np(v.dtype), kind="ExternalInput").ap()
            for name, v in arrays.items()]
    out = nc.dram_tensor("outT", (D, TOKENS), F32, kind="ExternalOutput").ap()
    adaln_ffn(nc, *args, out)
    result = run_bass_kernel_spmd(nc, [arrays], core_ids=[0])
    outT = np.asarray(result.results[0]["outT"])
    return np.ascontiguousarray(outT.T).reshape(BATCHES, T, D)
```

```python
from contextlib import ExitStack

import concourse.bass as bass
from concourse import mybir

F32 = mybir.dt.float32
F32R = mybir.dt.float32r
BF16 = mybir.dt.bfloat16
I32 = mybir.dt.int32
U32 = mybir.dt.uint32
ALU = mybir.AluOpType
ACT = mybir.ActivationFunctionType
AX_X = mybir.AxisListType.X

P = 128
D = 512
KT = D // P
F = 1376
FT = -(-F // P)
BATCHES, T = 128, 32
SLOTS, R = 32, 16
TOKENS = BATCHES * T
TN = 512
NT = TOKENS // TN
TILE_BATCHES = TN // T
LB = P // R
LN = LB * T
LG = TN // LN
LORA_SCALE = 2.0
NIBBLES = 8
GU_GROUPS = D // P
D_GROUPS = F // P
BANKS = 4
HI, MID, LO = 0, 32, 64
PARTS = 96
Q_SLOTS = 3
EARLY = 6
BEFORE_B = 6
LATE = 8
GATHER_CUTS = (KT - 2, 3, 4, 7, 10)
D_SLOTS = 2
SCALED = 2
DOWN_ORDER = [SCALED, *range(SCALED), *range(SCALED + 1, KT)]
RES_AT = 4
SPLIT_AT = 7
SPLIT_STEPS = 2
GATHER_AT = 4
GATHER_FIRST = 6
GATHER_SPLIT_AT = 6
LORA_AT = 9


def width(m):
    return min(P, F - m * P)


class BankOrder:

    def __init__(self):
        self.turn, self.fills, self.freed = 0, 0, [0] * BANKS
        self.parts = {}

    def add(self, part, names, repeats=1):
        assert repeats == 1 or len(names) % BANKS == 0
        places, uses, fills = {}, [0] * BANKS, 0
        for n, name in enumerate(names):
            bank = (self.turn + n) % BANKS
            if name is not None:
                fills += 1
                places[name] = (bank, self.fills + fills, self.freed[bank] + uses[bank])
                uses[bank] += 1
        self.parts[part] = (places, fills, uses)
        self.turn += len(names) * repeats
        self.fills += fills * repeats
        self.freed = [a + b * repeats for a, b in zip(self.freed, uses)]

    def bank(self, part, name):
        return self.parts[part][0][name][0]

    def filled(self, part, name, turn=0):
        places, fills, _ = self.parts[part]
        return turn * fills + places[name][1]

    def free(self, part, name, turn=0):
        places, _, uses = self.parts[part]
        bank, _, before = places[name]
        return turn * uses[bank] + before

    def taken(self, part, name, turn=0):
        return self.free(part, name, turn) + 1


def prologue_products():
    zero = [("zero", m, half) for m in range(FT) for half in range(2)]
    return zero[:2 * EARLY] + [("ranks",)] + zero[2 * EARLY:]


def tile_products(grouped, part):
    names = []
    for m in range(FT):
        if part == "first":
            names.append(("down zero", m))
        for g in range(GU_GROUPS if grouped else 1):
            names += [("gate", m, g), ("up", m, g)]
            if g == 0 and part == "first":
                names.append(("down scale", m))
            if grouped and DOWN_ORDER[g] < SCALED and (part != "first" or m >= 2):
                names.append(("down", m, DOWN_ORDER[g]))
        if m == LORA_AT and part != "last":
            names.append(("ranks",))
    if part == "loop":
        names += [None] * (-len(names + KT * [None]) % BANKS)
    if part != "last":
        names += [("cond", j) for j in range(KT)]
    elif grouped:
        names += [("down", m, j) for m in (FT, FT + 1) for j in range(SCALED)]
    return names


def h_tile_of(part, m):
    return m - 2 if m >= 2 else FT - 1 - m


def additions(t, part, m):
    if m < 0:
        return FT * t - 2 if part != "first" else 0
    done = min(m + 1, 2) + max(m - 2, 0) + (m > RES_AT)
    return FT * t - 2 + done if part != "first" else max(done - 2, 0)


def bank_order(grouped):
    order = BankOrder()
    order.add("prologue", prologue_products())
    if not grouped:
        order.add("weights", [(what, m, half) for m in range(FT) for half in range(2)
                              for what in ("zero", "scale")])
    order.add("first", tile_products(grouped, "first"))
    order.add("loop", tile_products(grouped, "loop"), NT - 2)
    order.add("last", tile_products(grouped, "last"))
    return order


def adaln_ffn(nc, xT, slots, wcT, bias, lora_a, lora_b, q_gu, q_gu_tail, qz_gu, s_gu, s_gu_col,
              s_gu_col_tail, gidx_gu, q_d, qz_d, s_d, s_d_col, gidx_d, outT):
    with ExitStack() as ctx:
        def sb(name, shape, dt=F32):
            return ctx.enter_context(nc.sbuf_tensor(name, shape, dt))

        def sem(name):
            return ctx.enter_context(nc.semaphore(name))

        gu_w = sb("gu_w", [P, FT, 2, KT, P], F32R)
        d_hi = sb("d_hi", [P, FT, D], F32R)
        d_lo = sb("d_lo", [P, FT, D], F32R)
        wc_hi = sb("wc_hi", [P, KT, D], F32R)
        wc_lo = sb("wc_lo", [P, KT, D], F32R)
        x_in = sb("x_in", [P, KT, TN])
        x_hi = sb("x_hi", [P, KT, TN], F32R)
        x_lo = sb("x_lo", [P, KT, TN], F32R)
        res = sb("res", [P, KT, TN])
        y_hi = sb("y_hi", [P, KT, TN], F32R)
        y_lo = sb("y_lo", [P, KT, TN], F32R)
        a_in = sb("a_in", [P, TILE_BATCHES, KT * R])
        a_hi = sb("a_hi", [P, LG, KT, P], F32R)
        a_lo = sb("a_lo", [P, LG, KT, P], F32R)
        b_in = sb("b_in", [P, LG, D])
        b_hi = sb("b_hi", [P, LG, D], F32R)
        b_lo = sb("b_lo", [P, LG, D], F32R)
        mask = sb("mask", [P, LB, T], BF16)
        ranks = sb("ranks", [P, TN])
        ranks_hi = sb("ranks_hi", [P, TN], F32R)
        ranks_lo = sb("ranks_lo", [P, TN], F32R)
        acc = sb("acc", [P, 2, 2, TN])
        h_hi = sb("h_hi", [P, 2, TN], F32R)
        h_lo = sb("h_lo", [P, 2, TN], F32R)
        q_d_sb = sb("q_d_sb", [P, D_SLOTS, D], U32)
        q_gu_sb = sb("q_gu_sb", [P, 2, KT * P], U32)
        w_new = sb("w_new", [P, D_SLOTS, D])
        member = sb("member", [PARTS, D + F], BF16)
        scratch = sb("scratch", [P, F])
        z_d = sb("z_d", [D_GROUPS, D], BF16)
        s_d_parts = sb("s_d_parts", [PARTS, D], BF16)
        s_col = sb("s_col", [P, FT, 2, GU_GROUPS])
        s_d_col_sb = sb("s_d_col_sb", [P, SCALED, D_GROUPS])
        bias_sb = sb("bias_sb", [P, KT])
        shift = sb("shift", [P, 1], U32)
        group = sb("group", [P, 1])
        slots_sb = sb("slots_sb", [1, BATCHES], I32)
        odd = sb("odd", [P, 1])
        odd_rows_i = sb("odd_rows_i", [1, 1], I32)
        column = sb("column", [P, 2], I32)

        gidx_sb = res[:].rearrange("p k n -> p (k n)").bitcast(I32)[0:PARTS, 0:D + F]
        gidx_float = gidx_sb.bitcast(F32)
        qz_gu_sb = ranks[0:GU_GROUPS, 0:2 * F // NIBBLES].bitcast(U32)
        FIRST_ROW, ROWS = 32, 65
        gidx_rows = ranks[:, 0:P].bitcast(I32)
        gu_rows, d_rows, last_rows = slice(32, 32 + GU_GROUPS), slice(64, 64 + FT - 1), slice(96, 97)
        odd_row = ranks[0:1, TN - ROWS:TN]
        qz_d_sb = ranks[0:D_GROUPS, TN - ROWS - D // NIBBLES:TN - ROWS].bitcast(U32)
        spare = [acc[:, i // 2, i % 2, :] for i in range(4)]
        z_d_tmp = spare[2].bitcast(U32)[0:D_GROUPS, :]
        scale_in = spare[3][0:PARTS, :]
        scale_rest = spare[2].bitcast(BF16)[0:PARTS, 0:D]
        s_gu_parts = spare[1].bitcast(BF16)[0:PARTS, 0:P]

        z_gu = scratch[0:GU_GROUPS, :].bitcast(BF16)
        unit = [scratch[:, j * TN:(j + 1) * TN] for j in range(SCALED)]
        early_sum = [q_gu_sb[:, j, :].bitcast(F32) for j in range(SCALED)]

        ring = ctx.enter_context(nc.psum_tensor("ring", [P, BANKS, TN], F32))
        down_ps = ctx.enter_context(nc.psum_tensor("down_ps", [P, KT, TN], F32))

        wc_in = [(q_gu_sb, q_d_sb)[k // 2][:, k % 2, :].bitcast(F32) for k in range(KT)]
        q_buffers = [buffer.rearrange("p a n -> p (a n)").bitcast(U32)
                     for buffer in (q_gu_sb, w_new, acc[:, 0], q_d_sb)]

        slots_loaded = sem("slots_loaded")
        gidx_gu_loaded = sem("gidx_gu_loaded")
        gidx_d_loaded = sem("gidx_d_loaded")
        qz_gu_loaded = sem("qz_gu_loaded")
        qz_d_loaded = sem("qz_d_loaded")
        s_d_loaded = sem("s_d_loaded")
        columns_loaded = sem("columns_loaded")
        wc_loaded = [sem(f"wc_loaded{k}") for k in range(KT)]
        x0_loaded = [sem(f"x0_loaded{k}") for k in range(KT)]
        x_loaded = sem("x_loaded")
        a_loaded = sem("a_loaded")
        b_loaded = sem("b_loaded")
        q_loaded = [sem(f"q_loaded{i}") for i in range(Q_SLOTS + 1)]
        qd_loaded = [sem(f"qd_loaded{i}") for i in range(D_SLOTS)]
        s_gu_loaded = sem("s_gu_loaded")
        added = [sem(f"added{j}") for j in range(SCALED)]
        w_moved = sem("w_moved")
        out_stored = sem("out_stored")
        scale_in_cleared = sem("scale_in_cleared")
        indices_made = sem("indices_made")
        odd_cleared = sem("odd_cleared")
        gidx_rows_loaded = sem("gidx_rows_loaded")
        odd_made = sem("odd_made")
        odd_moved = sem("odd_moved")
        constants_made = sem("constants_made")
        pool_step = sem("pool_step")
        mask_made = sem("mask_made")
        dve_step = sem("dve_step")
        gidx_d_float_made = sem("gidx_d_float_made")
        member_gu_made = sem("member_gu_made")
        member_d_made = sem("member_d_made")
        form_known = sem("form_known")
        zero_unpacked = sem("zero_unpacked")
        z_gu_made = sem("z_gu_made")
        z_d_made = sem("z_d_made")
        s_d_made = sem("s_d_made")
        s_gu_made = sem("s_gu_made")
        wc_hi_made = sem("wc_hi_made")
        wc_lo_made = sem("wc_lo_made")
        d_hi_made = sem("d_hi_made")
        d_lo_made = sem("d_lo_made")
        x_hi_made = sem("x_hi_made")
        x_lo_made = sem("x_lo_made")
        res_made = sem("res_made")
        adapters_hi_made = sem("adapters_hi_made")
        a_lo_made = sem("a_lo_made")
        b_lo_made = sem("b_lo_made")
        ranks_hi_made = sem("ranks_hi_made")
        ranks_lo_made = sem("ranks_lo_made")
        cond0_filled = sem("cond0_filled")
        y_hi_made = sem("y_hi_made")
        y0_made = sem("y0_made")
        silu_made = sem("silu_made")
        h_made = sem("h_made")
        h_hi_made = sem("h_hi_made")
        h_lo_made = sem("h_lo_made")
        h_used = sem("h_used")
        down_filled = sem("down_filled")
        out_made = sem("out_made")
        filled = sem("filled")
        taken = [sem(f"taken{b}") for b in range(BANKS)]

        SUMS = {True: range(SCALED, KT), False: range(KT)}
        STORES = {True: KT - SCALED + 1, False: KT}
        orders = {form: bank_order(form) for form in (True, False)}

        def in_both_forms(engine, run):
            engine.wait_ge(form_known, 1)
            odd = engine.value_load(odd_rows_i[0:1, 0:1], min_val=0, max_val=D + F)
            with engine.If(odd < 1):
                run(True)
            with engine.Else():
                run(False)

        def all_tiles(engine, run):
            run(0, "first", 0)
            with engine.Fori(1, NT - 1) as t:
                run(t, "loop", t - 1)
            run(NT - 1, "last", 0)

        def columns_of(half, m):
            return slice(half * F + m * P, half * F + m * P + width(m))

        def q_place(part, m):
            if part == "prologue":
                return m % Q_SLOTS, m // Q_SLOTS + 1
            slot = m % 2 * Q_SLOTS
            return slot, m // 2 + 1 + (len(range(0, FT, Q_SLOTS)) if slot == 0 else 0)

        def words(part, m):
            return q_buffers[q_place(part, m)[0]][:, 0:2 * KT * width(m)]

        def by_half(q):
            return q.rearrange("p (h k n) -> p h k n", h=2, k=KT)

        def split_of(part, m):
            n, step = KT // SPLIT_STEPS, m - SPLIT_AT
            return range(step * n, (step + 1) * n) if part != "last" and 0 <= step < SPLIT_STEPS else ()

        def gather(engine, t, batches=range(TILE_BATCHES)):
            for b in batches:
                slot = engine.value_load(slots_sb[0:1, bass.ds(t * TILE_BATCHES + b, 1)],
                                         min_val=0, max_val=SLOTS - 1)
                engine.dma_start(a_in[:, b, :], lora_a[bass.ds(slot, 1)].rearrange("o p c -> (o p) c")
                                 ).then_inc(a_loaded, 16)
                engine.dma_start(b_in[b % LB * R:(b % LB + 1) * R, b // LB, :],
                                 lora_b[bass.ds(slot, 1)].rearrange("o r n -> (o r) n")
                                 ).then_inc(b_loaded, 16)

        def make_member(engine, settle, columns, groups, made):
            clamp_groups(engine, settle, columns, groups)
            find_members(engine, columns, made)

        def clamp_groups(engine, settle, columns, groups):
            idx, wrap = gidx_float[:, columns], member[:, columns]
            settle(engine.tensor_scalar(wrap, idx, 0.0, float(groups), ALU.is_lt, ALU.mult))
            settle(engine.tensor_tensor(idx, idx, wrap, ALU.add))
            settle(engine.tensor_scalar(idx, idx, 0.0, float(groups - 1), ALU.max, ALU.min))

        def find_members(engine, columns, made):
            engine.tensor_scalar(member[:, columns], gidx_float[:, columns], group[0:PARTS, 0:1], None,
                                 ALU.is_equal).then_inc(made, 1)

        def side_by_side(ap, m):
            return ap.rearrange("p (k n) -> p k n", n=P)[:, :, 0:width(m)]

        def by_rank(ap):
            return ap.rearrange("p k (b r) -> p k b r", r=R)

        def by_slot(g):
            return a_in[:, g * LB:(g + 1) * LB, :].rearrange("p b (k r) -> p k b r", r=R)

        block = ctx.enter_context(nc.Block())

        @block.sync
        def _(sp):
            def load_x(t):
                sp.wait_ge(res_made, t)
                sp.dma_start(x_in[:], xT[:, bass.ds(t * TN, TN)].rearrange("(k p) n -> p k n", p=P)
                             ).then_inc(x_loaded, 16)

            def load_q(part, m):
                src = q_gu[m] if m < FT - 1 else q_gu_tail
                sp.dma_start(words(part, m),
                             src.unsqueeze(1).to_broadcast([P // NIBBLES, NIBBLES, src.shape[-1]])
                             ).then_inc(q_loaded[q_place(part, m)[0]], 16)

            def wait_taken(order, part, name):
                sp.wait_ge(taken[order.bank(part, name)], order.taken(part, name))

            def load_q_down(grouped, order, m):
                if m == 0 and not grouped:
                    wait_taken(order, "weights", ("zero", FT - 1, 1))
                if m >= D_SLOTS:
                    wait_taken(order, "first", ("down zero", m - D_SLOTS))
                rows = width(m) // NIBBLES
                src = q_d[m * P // NIBBLES:m * P // NIBBLES + rows, :]
                sp.dma_start(q_d_sb[0:width(m), m % D_SLOTS, :],
                             src.unsqueeze(1).to_broadcast([rows, NIBBLES, D])
                             ).then_inc(qd_loaded[m % D_SLOTS], 16)

            sp.dma_start(slots_sb[:], slots).then_inc(slots_loaded, 16)
            sp.dma_start(gidx_sb[:, 0:D], gidx_gu.to_broadcast([PARTS, D])).then_inc(gidx_gu_loaded, 16)
            for k in range(KT):
                sp.dma_start(x_in[:, k, :], xT[k * P:(k + 1) * P, 0:TN]).then_inc(x0_loaded[k], 16)
                sp.dma_start(wc_in[k], wcT[k * P:(k + 1) * P, :]).then_inc(wc_loaded[k], 16)
                if k == 0:
                    sp.dma_start(qz_gu_sb, qz_gu).then_inc(qz_gu_loaded, 16)
                    sp.wait_ge(slots_loaded, 16)
                elif k < KT - 1:
                    gather(sp, 0, [k - 1])
            sp.dma_start(gidx_sb[:, D:D + F], gidx_d.to_broadcast([PARTS, F])).then_inc(gidx_d_loaded, 16)
            sp.dma_start(gidx_rows[gu_rows], gidx_gu.rearrange("o (m p) -> (o m) p", p=P)
                         ).then_inc(gidx_rows_loaded, 16)
            sp.dma_start(gidx_rows[d_rows], gidx_d[:, 0:(FT - 1) * P].rearrange("o (m p) -> (o m) p", p=P)
                         ).then_inc(gidx_rows_loaded, 16)
            sp.dma_start(gidx_rows[last_rows, 0:width(FT - 1)], gidx_d[:, (FT - 1) * P:F]
                         ).then_inc(gidx_rows_loaded, 16)

            for m in range(FT):
                if m < len(GATHER_CUTS) - 1:
                    gather(sp, 0, range(GATHER_CUTS[m], GATHER_CUTS[m + 1]))
                if m == 0:
                    sp.wait_ge(wc_lo_made, 2)
                elif m == 2:
                    sp.wait_ge(z_gu_made, NIBBLES)
                elif m >= Q_SLOTS:
                    wait_taken(orders[True], "prologue", ("zero", m - Q_SLOTS, 1))
                load_q("prologue", m)
                if m == EARLY:
                    sp.dma_start(bias_sb[:], bias).then_inc(columns_loaded, 16)
                    sp.dma_start(s_d_col_sb[:], s_d_col).then_inc(columns_loaded, 16)
                    sp.dma_start(s_col[:, 0:FT - 1, :, :], s_gu_col).then_inc(columns_loaded, 16)
                    sp.dma_start(s_col[0:width(FT - 1), FT - 1, :, :], s_gu_col_tail
                                 ).then_inc(columns_loaded, 16)

            def tiles(grouped):
                order, split_from = orders[grouped], SUMS[grouped][0] * P

                if not grouped:
                    for m in range(FT):
                        if m == 0:
                            wait_taken(order, "prologue", ("zero", (FT - 1) // Q_SLOTS * Q_SLOTS, 1))
                        elif m >= 2:
                            wait_taken(order, "weights", ("zero", m - 2, 1))
                        load_q("weights", m)
                        for half in range(2):
                            i = 2 * m + half
                            if i == 0:
                                sp.wait_ge(s_d_made, 1)
                            else:
                                sp.wait_ge(s_gu_made, i)
                            for part in (HI, MID, LO):
                                sp.dma_start(scale_in[part:part + GU_GROUPS, 0:width(m)],
                                             s_gu[:, columns_of(half, m)]).then_inc(s_gu_loaded, 16)
                            wait_taken(order, "weights", ("scale", m, half))
                            sp.dma_start(gu_w[:, m, half, :, 0:width(m)].bitcast(F32),
                                         w_new[:, 0, 0:KT * width(m)].rearrange(
                                             "p (k n) -> p k n", k=KT)).then_inc(w_moved, 16)

                def store(t):
                    sums, tokens = SUMS[grouped], bass.ds(t * TN, TN)
                    if grouped:
                        for j in range(SCALED):
                            sp.wait_ge(added[j], FT * (t + 1))
                        sp.dma_start(outT[0:SCALED * P, tokens].rearrange("(k p) n -> p k n", p=P),
                                     res[:, 0:SCALED, :]).then_inc(out_stored, 16)
                    for i, j in enumerate(sums):
                        sp.wait_ge(out_made, len(sums) * t + i + 1)
                        sp.dma_start(outT[j * P:(j + 1) * P, tokens], res[:, j, :]).then_inc(out_stored, 16)

                def tile(t, part, turn):
                    if part == "first":
                        for m in range(FT):
                            load_q_down(grouped, order, m)
                            if m == 0:
                                sp.wait_ge(a_lo_made, LG)
                                sp.wait_ge(b_lo_made, LG)
                            if m * GATHER_AT < TILE_BATCHES:
                                gather(sp, 1, range(m * GATHER_AT, (m + 1) * GATHER_AT))
                            if m == RES_AT + D_SLOTS:
                                load_x(1)
                    else:
                        if part == "loop":
                            sp.wait_ge(a_lo_made, LG * (t + 1))
                            sp.wait_ge(b_lo_made, LG * (t + 1))
                            gather(sp, t + 1, range(GATHER_FIRST))
                        store(t - 1)
                        if part == "loop":
                            gather(sp, t + 1, range(GATHER_FIRST, TILE_BATCHES))
                            load_x(t + 1)
                    if part == "last":
                        store(t)

                all_tiles(sp, tile)
                sp.wait_ge(out_stored, 16 * STORES[grouped] * NT)

            in_both_forms(sp, tiles)

        @block.gpsimd
        def _(pool):
            pool.memset(scale_in, 0.0).then_inc(scale_in_cleared, 1)
            pool.iota(column[:, 0:1], [[0, 1]], base=0, channel_multiplier=1)
            pool.iota(column[:, 1:2], [[0, 1]], base=0, channel_multiplier=4).then_inc(indices_made, 1)
            pool.memset(odd[:], 0.0).then_inc(odd_cleared, 1)
            pool.memset(mask[:], LORA_SCALE).then_inc(mask_made, 1)
            pool.wait_ge(mask_made, 1)
            pool.affine_select(out=mask[:], in_=mask[:], compare_op=ALU.is_ge, fill=0.0, base=0,
                               pattern=[[-R, LB], [0, T]], channel_multiplier=1).then_inc(mask_made, 1)
            pool.wait_ge(mask_made, 2)
            pool.affine_select(out=mask[:], in_=mask[:], compare_op=ALU.is_ge, fill=0.0, base=R - 1,
                               pattern=[[R, LB], [0, T]], channel_multiplier=-1).then_inc(mask_made, 1)

            steps = [0]

            def settle(instruction):
                steps[0] += 1
                instruction.then_inc(pool_step, 1)
                pool.wait_ge(pool_step, steps[0])

            pool.wait_ge(constants_made, 1)
            pool.wait_ge(gidx_d_float_made, 1)
            clamp_groups(pool, settle, slice(D, D + F), D_GROUPS)

            def a_low(t, g):
                pool.wait_ge(adapters_hi_made, (LG + 1) * t + g + 1)
                pool.tensor_tensor(by_rank(a_lo[:, g]), by_slot(g), by_rank(a_hi[:, g].bitcast(F32)),
                                   ALU.subtract).then_inc(a_lo_made, 1)

            def b_low(t, g):
                pool.wait_ge(adapters_hi_made, (LG + 1) * (t + 1))
                pool.tensor_tensor(b_lo[:, g], b_in[:, g], b_hi[:, g].bitcast(F32),
                                   ALU.subtract).then_inc(b_lo_made, 1)

            def ranks_low(t):
                pool.wait_ge(ranks_hi_made, t + 1)
                pool.tensor_tensor(ranks_lo[:], ranks[:], ranks_hi[:].bitcast(F32),
                                   ALU.subtract).then_inc(ranks_lo_made, 1)

            for g in range(LG):
                a_low(0, g)
            find_members(pool, slice(D, D + F), member_d_made)
            ranks_low(0)

            def tiles(grouped):
                order, split_from = orders[grouped], SUMS[grouped][0] * P

                def first_product(m):
                    a, name = acc[0:width(m), m % 2], ("up", m, GU_GROUPS - 1)
                    pool.wait_ge(silu_made, m + 1)
                    pool.wait_ge(taken[order.bank("first", name)], order.taken("first", name))
                    pool.tensor_tensor(a[:, 1], a[:, 0], a[:, 1], ALU.mult).then_inc(h_made, 1)

                def h_low(t, m):
                    n = width(m)
                    pool.wait_ge(h_hi_made, FT * t + m + 1)
                    pool.tensor_tensor(h_lo[0:n, m % 2], acc[0:n, m % 2, 1], h_hi[0:n, m % 2].bitcast(F32),
                                       ALU.subtract).then_inc(h_lo_made, 1)

                def add(t, part, turn, m, j):
                    sum_so_far = early_sum[j] if 2 < m <= RES_AT else res[:, j, :]
                    before = additions(t, part, m - 1) + (m == RES_AT + 1)
                    if not (isinstance(before, int) and before == 0):
                        pool.wait_ge(added[j], before)
                    bank = order.bank(part, ("down", m, j))
                    pool.wait_ge(taken[bank], order.taken(part, ("down", m, j), turn))
                    pool.tensor_tensor(sum_so_far, sum_so_far, unit[j], ALU.add).then_inc(added[j], 1)

                def add_early(t, part, j):
                    pool.wait_ge(added[j], additions(t, part, RES_AT))
                    pool.wait_ge(res_made, t + 1)
                    pool.tensor_tensor(res[:, j, :], res[:, j, :], early_sum[j],
                                       ALU.add).then_inc(added[j], 1)

                def tile(t, part, turn):
                    for m in range(FT):
                        if m >= 1:
                            h_low(t, m - 1)
                        if grouped and m != 2 and (part != "first" or m > 2):
                            for j in range(SCALED):
                                if m == RES_AT + 1:
                                    add_early(t, part, j)
                                add(t, part, turn, m, j)
                        if part == "first":
                            n = width(m)
                            pool.wait_ge(d_hi_made, m + 1)
                            pool.tensor_tensor(d_lo[0:n, m, split_from:], w_new[0:n, m % D_SLOTS, split_from:],
                                               d_hi[0:n, m, split_from:].bitcast(F32),
                                               ALU.subtract).then_inc(d_lo_made, 1)
                        if part != "last" and 0 <= m - GATHER_SPLIT_AT < LG:
                            a_low(t + 1, m - GATHER_SPLIT_AT)
                        if part != "last" and 0 <= m - GATHER_SPLIT_AT - LG < LG:
                            b_low(t + 1, m - GATHER_SPLIT_AT - LG)
                        if grouped and part == "first":
                            first_product(m)
                        if part != "last" and m == LORA_AT:
                            ranks_low(t + 1)
                    h_low(t, FT - 1)
                    if grouped and part == "last":
                        for m in (FT, FT + 1):
                            for j in range(SCALED):
                                add(t, part, turn, m, j)

                all_tiles(pool, tile)

            in_both_forms(pool, tiles)

        @block.scalar
        def _(act):
            def a_high(t):
                act.wait_ge(a_loaded, 16 * TILE_BATCHES * (t + 1))
                for g in range(LG):
                    act.activation(by_rank(a_hi[:, g]), by_slot(g), ACT.Copy).then_inc(adapters_hi_made, 1)

            def b_high(t):
                act.wait_ge(b_loaded, 16 * TILE_BATCHES * (t + 1))
                act.activation(b_hi[:], b_in[:], ACT.Copy).then_inc(adapters_hi_made, 1)

            def ranks_high(order, part, turn, t):
                bank = order.bank(part, ("ranks",))
                act.wait_ge(taken[bank], order.taken(part, ("ranks",), turn))
                act.activation(ranks_hi[:], ranks[:], ACT.Copy).then_inc(ranks_hi_made, 1)

            def round_y(j, product):
                act.activation(y_hi[:, j, :], product, ACT.Identity,
                               bias=bias_sb[:, j:j + 1]).then_inc(y_hi_made, 1)

            def cond_high(order, part, turn, j):
                act.wait_ge(filled, order.filled(part, ("cond", j), turn))
                round_y(j, ring[:, order.bank(part, ("cond", j)), :])

            act.wait_ge(odd_cleared, 1)
            act.activation(odd[:], odd[:], ACT.Silu).then_inc(odd_cleared, 1)
            for k in range(KT):
                act.wait_ge(x0_loaded[k], 16)
                act.activation(x_hi[:, k, :], x_in[:, k, :], ACT.Copy).then_inc(x_hi_made, 1)
                act.wait_ge(wc_loaded[k], 16)
                act.activation(wc_hi[:, k, :], wc_in[k], ACT.Copy).then_inc(wc_hi_made, 1)
                if k == 1:
                    act.dma_start(qz_d_sb, qz_d).then_inc(qz_d_loaded, 16)
                    act.wait_ge(scale_in_cleared, 1)
                    for part in (HI, MID, LO):
                        act.dma_start(scale_in[part:part + D_GROUPS, :], s_d).then_inc(s_d_loaded, 16)
            act.wait_ge(gidx_d_loaded, 16)
            act.activation(gidx_float[:, D:D + F], gidx_sb[:, D:D + F], ACT.Copy
                           ).then_inc(gidx_d_float_made, 1)
            for n in range(NIBBLES):
                act.wait_ge(zero_unpacked, n + 1)
                act.activation(z_gu[:, n:2 * F:NIBBLES],
                               spare[n % 3].bitcast(U32)[0:GU_GROUPS, 0:2 * F // NIBBLES],
                               ACT.Copy, bias=1.0).then_inc(z_gu_made, 1)
            act.wait_ge(odd_made, 1)
            act.dma_start(odd_row, odd[FIRST_ROW:FIRST_ROW + ROWS, 0:1]).then_inc(odd_moved, 16)
            act.wait_ge(slots_loaded, 16)
            gather(act, 0, range(GATHER_CUTS[-1], TILE_BATCHES))
            a_high(0)
            b_high(0)
            ranks_high(orders[True], "prologue", 0, 0)
            act.wait_ge(columns_loaded, 64)
            for j in range(KT):
                act.wait_ge(cond0_filled, j + 1)
                round_y(j, down_ps[:, j, :])

            def tiles(grouped):
                order, split_from = orders[grouped], SUMS[grouped][0] * P

                def start_group(t, part, turn, m, half):
                    name = (("gate", "up")[half], m, 0)
                    bank, n = order.bank(part, name), width(m)
                    act.wait_ge(filled, order.filled(part, name, turn))
                    act.activation(acc[0:n, m % 2, half], ring[0:n, bank, :], ACT.Copy,
                                   scale=s_col[0:n, m, half, 0:1]).then_inc(taken[bank], 1)

                def take_unit(t, part, turn, m, j):
                    name, h_tile = ("down", m, j), h_tile_of(part, m)
                    bank, group = order.bank(part, name), min(h_tile, D_GROUPS - 1)
                    free = additions(t, part, -1 if m == 2 else m - 1)
                    if not (isinstance(free, int) and free == 0):
                        act.wait_ge(added[j], free)
                    act.wait_ge(filled, order.filled(part, name, turn))
                    act.activation(early_sum[j] if m == 2 else unit[j], ring[:, bank, :], ACT.Copy,
                                   scale=s_d_col_sb[:, j, group:group + 1]).then_inc(taken[bank], 1)

                def acc_free(t, part, m):
                    if m >= 2:
                        act.wait_ge(h_lo_made, FT * t + m - 1)
                    elif part != "first":
                        act.wait_ge(h_lo_made, FT * t)

                def silu(t, part, turn, m):
                    a = acc[0:width(m), m % 2, 0]
                    if grouped:
                        name = ("gate", m, GU_GROUPS - 1)
                        act.wait_ge(taken[order.bank(part, name)], order.taken(part, name, turn))
                        act.activation(a, a, ACT.Silu).then_inc(silu_made, 1)
                    else:
                        name = ("gate", m, 0)
                        bank = order.bank(part, name)
                        act.wait_ge(filled, order.filled(part, name, turn))
                        act.activation(a, ring[0:width(m), bank, :], ACT.Silu).then_inc(taken[bank], 1)

                def h_high(t, part, turn, m):
                    n = width(m)
                    if grouped:
                        act.wait_ge(h_made, FT * t + m + 1)
                    else:
                        name = ("up", m, 0)
                        act.wait_ge(taken[order.bank(part, name)], order.taken(part, name, turn))
                    if m >= 2:
                        act.wait_ge(h_used, (FT - 1) * t + m - 1)
                    elif part != "first":
                        if m == 0:
                            act.wait_ge(h_used, (FT - 1) * t)
                        else:
                            act.wait_ge(down_filled, len(SUMS[grouped]) * t)
                    act.activation(h_hi[0:n, m % 2], acc[0:n, m % 2, 1], ACT.Copy).then_inc(h_hi_made, 1)

                def copy_residual(t, part):
                    act.wait_ge(x_lo_made, KT * (t + 1))
                    if part == "first":
                        act.wait_ge(form_known, 1)
                    else:
                        act.wait_ge(out_stored, 16 * STORES[grouped] * t)
                    for k in range(KT):
                        c = act.activation(res[:, k, :], x_in[:, k, :], ACT.Copy)
                    c.then_inc(res_made, 1)

                def tile(t, part, turn):
                    for m in range(FT):
                        acc_free(t, part, m)
                        if grouped:
                            for half in range(2):
                                start_group(t, part, turn, m, half)
                        if m >= 1:
                            h_high(t, part, turn, m - 1)
                        if grouped and (part != "first" or m >= 2):
                            for j in range(SCALED):
                                take_unit(t, part, turn, m, j)
                        if part == "first":
                            n, name = width(m), ("down scale", m)
                            act.wait_ge(taken[order.bank(part, name)], order.taken(part, name))
                            act.activation(d_hi[0:n, m, split_from:], w_new[0:n, m % D_SLOTS, split_from:],
                                           ACT.Copy).then_inc(d_hi_made, 1)
                        if m == RES_AT:
                            copy_residual(t, part)
                        for k in split_of(part, m):
                            act.wait_ge(x_loaded, 16 * (t + 1))
                            act.activation(x_hi[:, k, :], x_in[:, k, :], ACT.Copy).then_inc(x_hi_made, 1)
                        if part != "last" and m == GATHER_SPLIT_AT:
                            a_high(t + 1)
                            b_high(t + 1)
                        silu(t, part, turn, m)
                        if part != "last" and m == LORA_AT:
                            ranks_high(order, part, turn, t + 1)
                    h_high(t, part, turn, FT - 1)
                    if grouped and part == "last":
                        for m in (FT, FT + 1):
                            for j in range(SCALED):
                                take_unit(t, part, turn, m, j)
                    if part != "last":
                        for j in range(KT):
                            cond_high(order, part, turn, j)

                all_tiles(act, tile)

            in_both_forms(act, tiles)

        @block.vector
        def _(dve):
            steps = [0]

            def settle(instruction):
                steps[0] += 1
                instruction.then_inc(dve_step, 1)
                dve.wait_ge(dve_step, steps[0])

            def split_scale(parts, made):
                n = parts.shape[-1]
                rest, s = scale_rest[:, 0:n], scale_in[:, 0:n]
                settle(dve.tensor_copy(parts, s))
                settle(dve.tensor_tensor(s, s, parts, ALU.subtract))
                settle(dve.tensor_copy(rest, s))
                settle(dve.tensor_copy(parts[MID:LO], rest[MID:LO]))
                settle(dve.tensor_tensor(s, s, rest, ALU.subtract))
                dve.tensor_copy(parts[LO:PARTS], s[LO:PARTS]).then_inc(made, 1)

            def unpack(q):
                settle(dve.tensor_scalar(q, q, shift[0:q.shape[0], 0:1], 15,
                                         ALU.logical_shift_right, ALU.bitwise_and))

            def x_low(k):
                dve.tensor_tensor(x_lo[:, k, :], x_in[:, k, :], x_hi[:, k, :].bitcast(F32),
                                  ALU.subtract).then_inc(x_lo_made, 1)

            def unpack_gate_up(part, m):
                slot, loads = q_place(part, m)
                dve.wait_ge(q_loaded[slot], 16 * loads)
                unpack(words(part, m))

            def zero_weights(m):
                order, part = orders[True], "prologue"
                unpack_gate_up(part, m)
                for half in range(2):
                    bank = order.bank(part, ("zero", m, half))
                    dve.wait_ge(filled, order.filled(part, ("zero", m, half)))
                    dve.tensor_tensor(gu_w[:, m, half, :, 0:width(m)], by_half(words(part, m))[:, half],
                                      side_by_side(ring[:, bank, :], m),
                                      ALU.subtract).then_inc(taken[bank], 1)

            def take_ranks(order, part, turn, t):
                bank = order.bank(part, ("ranks",))
                if part != "prologue":
                    dve.wait_ge(ranks_lo_made, t)
                dve.wait_ge(filled, order.filled(part, ("ranks",), turn))
                for g in range(LG):
                    r = dve.tensor_tensor(ranks[:, g * LN:(g + 1) * LN], ring[:, bank, g * LN:(g + 1) * LN],
                                          mask[:].rearrange("p b t -> p (b t)"), ALU.mult)
                r.then_inc(taken[bank], 1)

            def y_rest(t, j, product):
                dve.wait_ge(y_hi_made, KT * t + j + 1)
                return dve.scalar_tensor_tensor(y_lo[:, j, :], product, bias_sb[:, j:j + 1],
                                                y_hi[:, j, :].bitcast(F32), ALU.add, ALU.subtract)

            def cond_low(order, part, turn, t, j):
                bank = order.bank(part, ("cond", j))
                y_rest(t, j, ring[:, bank, :]).then_inc(taken[bank], 1)

            dve.wait_ge(indices_made, 1)
            settle(dve.tensor_scalar(column[:, 0:1], column[:, 0:1], 31, None, ALU.bitwise_and))
            dve.tensor_copy(group[:], column[:, 0:1])
            dve.tensor_scalar(shift[:], column[:, 1:2].bitcast(U32), 4 * (NIBBLES - 1), None,
                              ALU.bitwise_and).then_inc(constants_made, 1)
            dve.wait_ge(constants_made, 1)
            dve.wait_ge(gidx_gu_loaded, 16)
            settle(dve.tensor_copy(gidx_float[:, 0:D], gidx_sb[:, 0:D]))
            make_member(dve, settle, slice(0, D), GU_GROUPS, member_gu_made)

            for k in range(KT):
                dve.wait_ge(x_hi_made, k + 1)
                x_low(k)
                dve.wait_ge(wc_hi_made, k + 1)
                dve.tensor_tensor(wc_lo[:, k, :], wc_in[k], wc_hi[:, k, :].bitcast(F32),
                                  ALU.subtract).then_inc(wc_lo_made, 1)

            dve.wait_ge(gidx_rows_loaded, 48)
            dve.wait_ge(odd_cleared, 2)
            equal = gidx_rows.bitcast(F32)
            for rows in (gu_rows, d_rows):
                dve.tensor_scalar(equal[rows], gidx_rows[rows], group[rows, 0:1], None, ALU.not_equal)
            settle(dve.tensor_scalar(equal[last_rows, 0:width(FT - 1)],
                                     gidx_rows[last_rows, 0:width(FT - 1)], float(D_GROUPS - 1), None,
                                     ALU.is_lt))
            for rows in (gu_rows, d_rows):
                dve.reduce_sum(odd[rows], equal[rows], axis=AX_X)
            dve.reduce_sum(odd[last_rows], equal[last_rows, 0:width(FT - 1)],
                           axis=AX_X).then_inc(odd_made, 1)

            dve.wait_ge(qz_gu_loaded, 16)
            for n in range(NIBBLES):
                if n >= 3:
                    dve.wait_ge(z_gu_made, n - 2)
                dve.tensor_scalar(spare[n % 3].bitcast(U32)[0:GU_GROUPS, 0:2 * F // NIBBLES],
                                  qz_gu_sb, 4 * n, 15, ALU.logical_shift_right,
                                  ALU.bitwise_and).then_inc(zero_unpacked, 1)
            dve.wait_ge(z_gu_made, NIBBLES)

            dve.wait_ge(qz_d_loaded, 16)
            z_columns = z_d_tmp.rearrange("g (c n) -> g c n", n=NIBBLES)
            for n in range(NIBBLES):
                z = dve.tensor_scalar(z_columns[:, :, n], qz_d_sb, 4 * n, 15, ALU.logical_shift_right,
                                      ALU.bitwise_and)
            settle(z)
            dve.tensor_scalar(z_d[:], z_d_tmp, 1.0, None, ALU.add).then_inc(z_d_made, 1)
            dve.wait_ge(z_d_made, 1)
            dve.wait_ge(s_d_loaded, 48)
            split_scale(s_d_parts[:], s_d_made)
            for m in range(Q_SLOTS):
                zero_weights(m)
            dve.wait_ge(odd_moved, 16)
            settle(dve.reduce_sum(odd[0:1], odd_row, axis=AX_X))
            dve.tensor_copy(odd_rows_i[:], odd[0:1]).then_inc(form_known, 1)

            for m in range(Q_SLOTS, EARLY):
                zero_weights(m)
            dve.wait_ge(mask_made, 3)
            take_ranks(orders[True], "prologue", 0, 0)
            for m in range(EARLY, BEFORE_B):
                zero_weights(m)
            dve.wait_ge(adapters_hi_made, LG + 1)
            for g in range(LG):
                dve.tensor_tensor(b_lo[:, g], b_in[:, g], b_hi[:, g].bitcast(F32),
                                  ALU.subtract).then_inc(b_lo_made, 1)
            for m in range(BEFORE_B, LATE):
                zero_weights(m)
            dve.wait_ge(columns_loaded, 64)
            for j in range(KT):
                y_rest(0, j, down_ps[:, j, :]).then_inc(y0_made, 1)
            for m in range(LATE, FT):
                zero_weights(m)
            before_forms = steps[0]

            def tiles(grouped):
                order, split_from = orders[grouped], SUMS[grouped][0] * P
                steps[0] = before_forms

                if not grouped:
                    for m in range(FT):
                        n = width(m)
                        unpack_gate_up("weights", m)
                        for half in range(2):
                            i = 2 * m + half
                            dve.wait_ge(s_gu_loaded, 48 * (i + 1))
                            split_scale(s_gu_parts[:, 0:n], s_gu_made)
                            if i >= 1:
                                dve.wait_ge(w_moved, 16 * i)
                            w = w_new[:, 0, 0:KT * n].rearrange("p (k n) -> p k n", k=KT)
                            zero = order.bank("weights", ("zero", m, half))
                            dve.wait_ge(filled, order.filled("weights", ("zero", m, half)))
                            dve.tensor_tensor(w, by_half(words("weights", m))[:, half],
                                              side_by_side(ring[:, zero, :], m),
                                              ALU.subtract).then_inc(taken[zero], 1)
                            scale = order.bank("weights", ("scale", m, half))
                            dve.wait_ge(taken[zero], order.taken("weights", ("zero", m, half)))
                            dve.wait_ge(filled, order.filled("weights", ("scale", m, half)))
                            dve.tensor_tensor(w, w, side_by_side(ring[:, scale, :], m),
                                              ALU.mult).then_inc(taken[scale], 1)

                def down_weights(m):
                    n = width(m)
                    zero, scale = [order.bank("first", (what, m)) for what in ("down zero", "down scale")]
                    q, w = q_d_sb[0:n, m % D_SLOTS], w_new[0:n, m % D_SLOTS]
                    dve.wait_ge(qd_loaded[m % D_SLOTS], 16 * (m // D_SLOTS + 1))
                    unpack(q)
                    if m >= D_SLOTS:
                        dve.wait_ge(d_lo_made, m - D_SLOTS + 1)
                    elif m == 0 and not grouped:
                        dve.wait_ge(w_moved, 16 * 2 * FT)
                    dve.wait_ge(filled, order.filled("first", ("down zero", m)))
                    if grouped:
                        dve.tensor_tensor(d_hi[0:n, m, 0:split_from], q[:, 0:split_from],
                                          ring[0:n, zero, 0:split_from], ALU.subtract)
                    w, q = w[:, split_from:], q[:, split_from:]
                    dve.tensor_tensor(w, q, ring[0:n, zero, split_from:],
                                      ALU.subtract).then_inc(taken[zero], 1)
                    dve.wait_ge(taken[zero], order.taken("first", ("down zero", m)))
                    dve.wait_ge(filled, order.filled("first", ("down scale", m)))
                    dve.tensor_tensor(w, w, ring[0:n, scale, split_from:],
                                      ALU.mult).then_inc(taken[scale], 1)

                def add_group(part, turn, m, half, g):
                    what, n = ("gate", "up")[half], width(m)
                    bank, last = order.bank(part, (what, m, g)), order.bank(part, (what, m, g - 1))
                    a = acc[0:n, m % 2, half]
                    dve.wait_ge(taken[last], order.taken(part, (what, m, g - 1), turn))
                    dve.wait_ge(filled, order.filled(part, (what, m, g), turn))
                    dve.scalar_tensor_tensor(a, ring[0:n, bank, :], s_col[0:n, m, half, g:g + 1], a,
                                             ALU.mult, ALU.add).then_inc(taken[bank], 1)

                def product(part, turn, m):
                    n = width(m)
                    gate, up = [order.bank(part, (what, m, 0)) for what in ("gate", "up")]
                    dve.wait_ge(taken[gate], order.taken(part, ("gate", m, 0), turn))
                    dve.wait_ge(filled, order.filled(part, ("up", m, 0), turn))
                    dve.tensor_tensor(acc[0:n, m % 2, 1], acc[0:n, m % 2, 0], ring[0:n, up, :],
                                      ALU.mult).then_inc(taken[up], 1)

                def scaled_product(t, part, turn, m):
                    a = acc[0:width(m), m % 2]
                    name = ("up", m, GU_GROUPS - 1)
                    dve.wait_ge(silu_made, FT * t + m + 1)
                    dve.wait_ge(taken[order.bank(part, name)], order.taken(part, name, turn))
                    dve.tensor_tensor(a[:, 1], a[:, 0], a[:, 1], ALU.mult).then_inc(h_made, 1)

                def output(t, j):
                    sums = SUMS[grouped]
                    if j == sums[0]:
                        dve.wait_ge(res_made, t + 1)
                    dve.wait_ge(down_filled, len(sums) * t + j - sums[0] + 1)
                    dve.tensor_tensor(res[:, j, :], res[:, j, :], down_ps[:, j, :],
                                      ALU.add).then_inc(out_made, 1)

                def tile(t, part, turn):
                    for m in range(FT):
                        if grouped and m >= 1 and part != "first":
                            scaled_product(t, part, turn, m - 1)
                        if part == "first":
                            down_weights(m)
                        if grouped:
                            for g in range(1, GU_GROUPS):
                                for half in range(2):
                                    add_group(part, turn, m, half, g)
                                if part != "first" and g == 1 and SCALED + m - 1 in SUMS[True] and m >= 1:
                                    output(t - 1, SCALED + m - 1)
                        else:
                            product(part, turn, m)
                            if part != "first" and m == 1:
                                for j in range(KT):
                                    output(t - 1, j)
                        for k in split_of(part, m):
                            dve.wait_ge(x_hi_made, KT * (t + 1) + k + 1)
                            x_low(k)
                        if part != "last" and m == LORA_AT:
                            take_ranks(order, part, turn, t + 1)
                    if grouped and part != "first":
                        scaled_product(t, part, turn, FT - 1)
                    if part != "last":
                        for j in range(KT):
                            cond_low(order, part, turn, t + 1, j)
                    else:
                        for j in SUMS[grouped]:
                            output(t, j)

                all_tiles(dve, tile)

            in_both_forms(dve, tiles)

        @block.tensor
        def _(pe):
            def wait_free(order, part, name, turn=0):
                bank, before = order.bank(part, name), order.free(part, name, turn)
                if not (isinstance(before, int) and before == 0):
                    pe.wait_ge(taken[bank], before)
                return bank

            def split_product(out, w_hi, w_lo, v_hi, v_lo, start, stop):
                pe.matmul(out, w_hi, v_hi, start=start, stop=False)
                pe.matmul(out, w_hi, v_lo, start=False, stop=False)
                return pe.matmul(out, w_lo, v_hi, start=False, stop=stop)

            def ranks_product(order, part, turn, t):
                bank = wait_free(order, part, ("ranks",), turn)
                pe.wait_ge(x_lo_made, KT * (t + 1))
                for g in range(LG):
                    pe.wait_ge(a_lo_made, LG * t + g + 1)
                    tokens = slice(g * LN, (g + 1) * LN)
                    for k in range(KT):
                        mm = split_product(ring[:, bank, tokens], a_hi[:, g, k], a_lo[:, g, k],
                                           x_hi[:, k, tokens], x_lo[:, k, tokens], k == 0, k == KT - 1)
                mm.then_inc(filled, 1)

            def adapter_product(out, j):
                columns = slice(j * P, (j + 1) * P)
                for g in range(LG):
                    tokens = slice(g * LN, (g + 1) * LN)
                    split_product(out[:, tokens], b_hi[:, g, columns], b_lo[:, g, columns],
                                  ranks_hi[:, tokens], ranks_lo[:, tokens], False, False)

            def cond_product(order, part, turn, t, j):
                bank = wait_free(order, part, ("cond", j), turn)
                columns = slice(j * P, (j + 1) * P)
                if j == 0:
                    pe.wait_ge(ranks_lo_made, t + 1)
                    pe.wait_ge(b_lo_made, LG * (t + 1))
                for k in range(KT):
                    mm = split_product(ring[:, bank, :], wc_hi[:, k, columns], wc_lo[:, k, columns],
                                       x_hi[:, k, :], x_lo[:, k, :], k == 0, k == KT - 1)
                    if k == 0:
                        adapter_product(ring[:, bank, :], j)
                mm.then_inc(filled, 1)

            def zero_product(order, part, m, half):
                bank = wait_free(order, part, ("zero", m, half))
                for k in range(KT):
                    mm = pe.matmul(ring[:, bank, k * P:k * P + width(m)],
                                   member[0:GU_GROUPS, k * P:(k + 1) * P], z_gu[:, columns_of(half, m)],
                                   start=True, stop=True)
                mm.then_inc(filled, 1)

            def wc_lo_product(j, k, stop):
                return pe.matmul(down_ps[:, j, :], wc_lo[:, k, j * P:(j + 1) * P], x_hi[:, k, :],
                                 start=False, stop=stop)

            for k in range(KT):
                if k == KT - 1:
                    pe.wait_ge(member_gu_made, 1)
                    pe.wait_ge(z_gu_made, NIBBLES)
                    for m in range(2):
                        for half in range(2):
                            zero_product(orders[True], "prologue", m, half)
                pe.wait_ge(wc_lo_made, k + 1)
                for j in range(KT):
                    w = wc_hi[:, k, j * P:(j + 1) * P]
                    pe.matmul(down_ps[:, j, :], w, x_hi[:, k, :], start=(k == 0), stop=False)
                    pe.matmul(down_ps[:, j, :], w, x_lo[:, k, :], start=False, stop=False)
                    if k < KT - 1:
                        wc_lo_product(j, k, False)
            for m in range(2, EARLY):
                for half in range(2):
                    zero_product(orders[True], "prologue", m, half)
            ranks_product(orders[True], "prologue", 0, 0)
            for m in range(EARLY, LATE):
                for half in range(2):
                    zero_product(orders[True], "prologue", m, half)
            pe.wait_ge(ranks_lo_made, 1)
            pe.wait_ge(b_lo_made, LG)
            for j in range(KT):
                adapter_product(down_ps[:, j, :], j)
                wc_lo_product(j, KT - 1, True).then_inc(cond0_filled, 1)
            for m in range(LATE, FT):
                for half in range(2):
                    zero_product(orders[True], "prologue", m, half)

            def tiles(grouped):
                order, split_from = orders[grouped], SUMS[grouped][0] * P
                pe.wait_ge(y0_made, KT)

                if not grouped:
                    for m in range(FT):
                        for half in range(2):
                            zero_product(order, "weights", m, half)
                            bank = wait_free(order, "weights", ("scale", m, half))
                            pe.wait_ge(s_gu_made, 2 * m + half + 1)
                            for k in range(KT):
                                mm = pe.matmul(ring[:, bank, k * P:k * P + width(m)],
                                               member[:, k * P:(k + 1) * P], s_gu_parts[:, 0:width(m)],
                                               start=True, stop=True)
                            mm.then_inc(filled, 1)
                    pe.wait_ge(w_moved, 16 * 2 * FT)

                def down_weight_product(what, m):
                    rows = slice(D + m * P, D + m * P + width(m))
                    bank = wait_free(order, "first", (what, m))
                    if m == 0:
                        pe.wait_ge(member_d_made, 1)
                        pe.wait_ge(s_d_made, 1)
                    if what == "down zero":
                        pe.matmul(ring[0:width(m), bank, :], member[0:D_GROUPS, rows], z_d[:],
                                  start=True, stop=True).then_inc(filled, 1)
                    else:
                        pe.matmul(ring[0:width(m), bank, split_from:], member[:, rows],
                                  s_d_parts[:, split_from:], start=True, stop=True).then_inc(filled, 1)

                def group_product(part, turn, m, half, g):
                    name, n = (("gate", "up")[half], m, g), width(m)
                    bank = wait_free(order, part, name, turn)
                    w = gu_w[:, m, half, g, 0:n]
                    pe.matmul(ring[0:n, bank, :], w, y_hi[:, g, :], start=True, stop=False)
                    pe.matmul(ring[0:n, bank, :], w, y_lo[:, g, :], start=False,
                              stop=True).then_inc(filled, 1)

                def general_product(part, turn, m, half):
                    name, n = (("gate", "up")[half], m, 0), width(m)
                    bank = wait_free(order, part, name, turn)
                    for k in range(KT):
                        w = gu_w[:, m, half, k, 0:n].bitcast(F32)
                        pe.matmul(ring[0:n, bank, :], w, y_hi[:, k, :].bitcast(F32),
                                  start=(k == 0), stop=False)
                        mm = pe.matmul(ring[0:n, bank, :], w, y_lo[:, k, :].bitcast(F32),
                                       start=False, stop=(k == KT - 1))
                    mm.then_inc(filled, 1)

                def down_product(t, part, turn, step, js):
                    m, sums = h_tile_of(part, step), SUMS[grouped]
                    of_tile, n = (t if step >= 2 else t - 1), width(m)
                    final = step in (1, FT + 1)
                    if len(js) == KT or js[0] == DOWN_ORDER[0]:
                        pe.wait_ge(h_lo_made, FT * of_tile + m + 1)
                        if part == "first":
                            pe.wait_ge(d_lo_made, m + 1)
                    for j in js:
                        columns = slice(j * P, (j + 1) * P)
                        if j not in sums:
                            bank = wait_free(order, part, ("down", step, j), turn)
                            w = d_hi[0:n, m, columns]
                            pe.matmul(ring[:, bank, :], w, h_hi[0:n, m % 2], start=True, stop=False)
                            pe.matmul(ring[:, bank, :], w, h_lo[0:n, m % 2], start=False,
                                      stop=True).then_inc(filled, 1)
                            continue
                        if m == 0 and part != "first":
                            pe.wait_ge(out_made, len(sums) * (t - 1) + j - sums[0] + 1)
                        mm = split_product(down_ps[:, j, :], d_hi[0:n, m, columns], d_lo[0:n, m, columns],
                                           h_hi[0:n, m % 2], h_lo[0:n, m % 2], m == 0, final)
                        if final:
                            mm.then_inc(down_filled, 1)
                    if not final and js[-1] == KT - 1:
                        mm.then_inc(h_used, 1)

                def tile(t, part, turn):
                    for m in range(FT):
                        if part == "first":
                            down_weight_product("down zero", m)
                            if grouped:
                                for half in range(2):
                                    name = ("zero", m, half)
                                    pe.wait_ge(taken[order.bank("prologue", name)],
                                               order.taken("prologue", name))
                        if grouped:
                            for g in range(GU_GROUPS):
                                for half in range(2):
                                    group_product(part, turn, m, half, g)
                                if part == "first" and g == 0:
                                    down_weight_product("down scale", m)
                                if part != "first" or m >= 2:
                                    down_product(t, part, turn, m, [DOWN_ORDER[g]])
                        else:
                            for half in range(2):
                                general_product(part, turn, m, half)
                            if part == "first":
                                down_weight_product("down scale", m)
                            if part != "first" or m >= 2:
                                down_product(t, part, turn, m, range(KT))
                        if part != "last" and m == LORA_AT:
                            ranks_product(order, part, turn, t + 1)
                    if part != "last":
                        for j in range(KT):
                            cond_product(order, part, turn, t + 1, j)
                        if part == "first":
                            pe.wait_ge(d_lo_made, FT)
                        if not grouped:
                            for j in range(KT):
                                name = ("cond", j)
                                pe.wait_ge(taken[order.bank(part, name)], order.taken(part, name, turn))
                    else:
                        for m in (FT, FT + 1):
                            down_product(t, part, turn, m, DOWN_ORDER if grouped else range(KT))

                all_tiles(pe, tile)

            in_both_forms(pe, tiles)


def kernel(**inputs):
    import numpy as np
    import concourse.bacc as bacc
    from concourse.bass_utils import run_bass_kernel_spmd

    a = {name: np.asarray(v) for name, v in inputs.items()}
    full = (FT - 1) * P
    q_gu = a["L0_ffn_qweight_gu"].reshape(KT, P // NIBBLES, 2, F).transpose(1, 2, 0, 3)
    s_gu = a["L0_ffn_scales_gu"].reshape(GU_GROUPS, 2, F)
    arrays = {
        "xT": a["x"].reshape(TOKENS, D).T,
        "slots": a["itok_B_0_23"].reshape(1, BATCHES),
        "wcT": a["L0_cond_W"].T,
        "bias": a["L0_cond_b"].reshape(KT, P).T,
        "lora_a": a["L0_cond_lora_As"].reshape(SLOTS, KT, P, R).transpose(0, 2, 1, 3).reshape(
            SLOTS, P, KT * R),
        "lora_b": a["L0_cond_lora_Bs"],
        "q_gu": q_gu[..., :full].reshape(P // NIBBLES, 2, KT, FT - 1, P).transpose(3, 0, 1, 2, 4).reshape(
            FT - 1, P // NIBBLES, 2 * KT * P),
        "q_gu_tail": q_gu[..., full:].reshape(P // NIBBLES, -1),
        "qz_gu": a["L0_ffn_qzeros_gu"],
        "s_gu": a["L0_ffn_scales_gu"],
        "s_gu_col": s_gu[..., :full].reshape(GU_GROUPS, 2, FT - 1, P).transpose(3, 2, 1, 0),
        "s_gu_col_tail": s_gu[..., full:].transpose(2, 1, 0),
        "gidx_gu": a["L0_ffn_g_idx_gu"].reshape(1, D),
        "q_d": a["L0_ffn_qweight_down"],
        "qz_d": a["L0_ffn_qzeros_down"],
        "s_d": a["L0_ffn_scales_down"],
        "s_d_col": a["L0_ffn_scales_down"].reshape(D_GROUPS, KT, P)[:, :SCALED].transpose(2, 1, 0),
        "gidx_d": a["L0_ffn_g_idx_down"].reshape(1, F),
    }
    arrays = {name: np.ascontiguousarray(v) for name, v in arrays.items()}
    nc = bacc.Bacc("TRN2", target_bir_lowering=False, num_devices=1, dynamic_dma_scratch_size=1024)
    args = [nc.dram_tensor(name, v.shape, mybir.dt.from_np(v.dtype), kind="ExternalInput").ap()
            for name, v in arrays.items()]
    out = nc.dram_tensor("outT", (D, TOKENS), F32, kind="ExternalOutput").ap()
    adaln_ffn(nc, *args, out)
    result = run_bass_kernel_spmd(nc, [arrays], core_ids=[0])
    outT = np.asarray(result.results[0]["outT"])
    return np.ascontiguousarray(outT.T).reshape(BATCHES, T, D)
```
